# Optimizing a Trainium2 kernel written in Bass

```python
import numpy as np
import jax
import jax.numpy as jnp

def _softmax(x, axis=-1):
    return jax.nn.softmax(x, axis=axis)

def _gelu(x):
    return jax.nn.gelu(x, approximate=True)

def _silu(x):
    return jax.nn.silu(x)

def _sigmoid(x):
    return jax.nn.sigmoid(x)

def _layernorm(x, axis=-1, eps=1e-05):
    m = jnp.mean(x, axis=axis, keepdims=True)
    v = jnp.var(x, axis=axis, keepdims=True)
    return (x - m) / jnp.sqrt(v + eps)

def _scatter_add(tgt, idx, src, axis=0):
    return tgt.at[idx].add(src)

def _segment_sum(src, seg, n):
    return jax.ops.segment_sum(src, seg, n)
kernel_name = 'mk_gnn_preln_d4_gnn_r8_0ef0f4'

def setup_inputs(seed: int=0):
    np.random.seed(seed)
    _w = jnp.asarray

    def _rec_inputs():
        import jax
        import jax.numpy as jnp
        _gk = jax.random.key(seed)
        x = -0.000202 + 1 * jax.random.normal(jax.random.fold_in(_gk, 1), (6250, 128), jnp.float32)
        _s = jax.random.randint(jax.random.fold_in(_gk, 2), (100000,), 0, 6250, jnp.int32)
        _d = jax.random.randint(jax.random.fold_in(_gk, 3), (100000,), 0, 6250, jnp.int32)
        _loop = jnp.arange(6250, dtype=jnp.int32)
        src = jnp.concatenate([_s, _d, _loop])
        dst = jnp.concatenate([_d, _s, _loop])
        _o = jnp.argsort(dst, stable=True)
        src = src[_o]
        dst = dst[_o]
        edge_attr_128 = -5.16925e-05 + 1.00005 * jax.random.normal(jax.random.fold_in(_gk, 12), (206250, 128), jnp.float32)
        edge_attr_128_n2 = -5.16925e-05 + 1.00005 * jax.random.normal(jax.random.fold_in(_gk, 13), (206250, 128), jnp.float32)
        return (x, src, dst, edge_attr_128, edge_attr_128_n2)
    x, src, dst, edge_attr_128, edge_attr_128_n2 = _rec_inputs()

    def _L0_gnn_setup():
        import jax, jax.numpy as jnp
        import numpy as np
        N, F_IN, C_OUT, H = (6250, 128, 32, 4)
        ALPHA = 0.5
        SLOPE = 0.2

        def _gat_conv(x, W, a_src, a_dst, b, src, dst):
            n = x.shape[0]
            h = (x @ W).reshape(n, H, C_OUT)
            e_src = jnp.sum(h * a_src[None], -1)
            e_dst = jnp.sum(h * a_dst[None], -1)
            e = jax.nn.leaky_relu(e_src[src] + e_dst[dst], SLOPE)
            m = jax.ops.segment_max(e, dst, num_segments=n)
            ex = jnp.exp(e - m[dst])
            denom = jax.ops.segment_sum(ex, dst, num_segments=n)
            att = ex / denom[dst]
            msg = h[src] * att[:, :, None]
            out = jax.ops.segment_sum(msg, dst, num_segments=n)
            return out.reshape(n, H * C_OUT) + b
        key = jax.random.key(seed)
        ks = jax.random.split(key, 12)
        x = jax.random.normal(ks[0], (N, F_IN), dtype=jnp.float32)
        edge_index = jax.random.randint(ks[1], (2, 200000), 0, N, dtype=jnp.int64)

        def gat_params(k):
            k1, k2, k3, k4 = jax.random.split(k, 4)
            W = jax.random.normal(k1, (F_IN, H * C_OUT), dtype=jnp.float32) * 0.1
            a_src = jax.random.normal(k2, (H, C_OUT), dtype=jnp.float32) * 0.1
            a_dst = jax.random.normal(k3, (H, C_OUT), dtype=jnp.float32) * 0.1
            b = jax.random.normal(k4, (H * C_OUT,), dtype=jnp.float32) * 0.1
            return (W, a_src, a_dst, b)
        W1, a_src1, a_dst1, b1 = gat_params(ks[2])
        W2, a_src2, a_dst2, b2 = gat_params(ks[3])
        return {'x': x, 'edge_index': edge_index, 'W1': W1, 'a_src1': a_src1, 'a_dst1': a_dst1, 'b1': b1, 'W2': W2, 'a_src2': a_src2, 'a_dst2': a_dst2, 'b2': b2}
    _L0_gnn_all = _L0_gnn_setup()
    _L0_gnn_in = {k: v for k, v in _L0_gnn_all.items() if k in ('W1', 'a_src1', 'a_dst1', 'b1', 'W2', 'a_src2', 'a_dst2', 'b2')}
    del _L0_gnn_all

    def _L1_gnn_setup():
        import jax, jax.numpy as jnp
        import numpy as np
        EPS = 1e-12
        key = jax.random.key(seed)
        k1, k2, k3, k4, k5 = jax.random.split(key, 5)
        N, E, D_IN, D_OUT = (12500, 200000, 128, 128)
        features = jax.random.normal(k1, (N, D_IN), dtype=jnp.float32)
        W = jax.random.normal(k2, (D_OUT, D_IN), dtype=jnp.float32) * 0.05
        b = jax.random.normal(k3, (D_OUT,), dtype=jnp.float32) * 0.05
        src = jax.random.randint(k4, (E,), 0, N, dtype=jnp.int32)
        dst = jax.random.randint(k5, (E,), 0, N, dtype=jnp.int32)
        return {'features': features, 'W': W, 'b': b, 'src': src, 'dst': dst}
    _L1_gnn_all = _L1_gnn_setup()
    _L1_gnn_in = {k: v for k, v in _L1_gnn_all.items() if k in ('W', 'b')}
    del _L1_gnn_all

    def _L2_gnn_setup():
        import jax, jax.numpy as jnp
        import numpy as np
        N = 6250
        E = 75000
        IN = 128
        H = 4
        C = 32
        B = 3
        NEG_SLOPE = 0.2
        key = jax.random.key(seed)
        ks = jax.random.split(key, 6)
        x = jax.random.normal(ks[0], (N, IN), dtype=jnp.float32)
        edge_index = jax.random.randint(ks[1], (2, E), 0, N)
        coeffs_t = jnp.array([0.25, 0.5, 0.25], dtype=jnp.float32)
        glorot_w = float(np.sqrt(2.0) * np.sqrt(6.0 / (H * C + IN)))
        glorot_a = float(np.sqrt(2.0) * np.sqrt(6.0 / (1 + C)))
        lin_weight = jax.random.uniform(ks[2], (B, H * C, IN), jnp.float32, -glorot_w, glorot_w)
        lin_bias = jnp.zeros((B, H * C), dtype=jnp.float32)
        att_src = jax.random.uniform(ks[3], (B, 1, H, C), jnp.float32, -glorot_a, glorot_a)
        att_dst = jax.random.uniform(ks[4], (B, 1, H, C), jnp.float32, -glorot_a, glorot_a)
        return {'x': x, 'edge_index': edge_index, 'coeffs_t': coeffs_t, 'lin_weight': lin_weight, 'lin_bias': lin_bias, 'att_src': att_src, 'att_dst': att_dst}
    _L2_gnn_all = _L2_gnn_setup()
    _L2_gnn_in = {k: v for k, v in _L2_gnn_all.items() if k in ('coeffs_t', 'lin_weight', 'lin_bias', 'att_src', 'att_dst')}
    del _L2_gnn_all

    def _L3_gnn_setup():
        import jax, jax.numpy as jnp
        import numpy as np
        DIM, HEADS = (128, 8)
        DH = DIM // HEADS
        SCALE = DH ** (-0.5)
        N, E = (6250, 100000)
        key = jax.random.key(seed)
        ks = jax.random.split(key, 12)
        w = lambda k: jax.random.normal(k, (DIM, DIM), dtype=jnp.float32) * 0.02
        b = lambda k: jax.random.normal(k, (DIM,), dtype=jnp.float32) * 0.02
        return {'q_nodes': jax.random.normal(ks[0], (N, DIM), dtype=jnp.float32), 'k_edges': jax.random.normal(ks[1], (E, DIM), dtype=jnp.float32), 'v_edges': jax.random.normal(ks[2], (E, DIM), dtype=jnp.float32), 'edge_index': jax.random.randint(ks[3], (2, E), 0, N, dtype=jnp.int64), 'Wq': w(ks[4]), 'bq': b(ks[5]), 'Wk': w(ks[6]), 'bk': b(ks[7]), 'Wv': w(ks[8]), 'bv': b(ks[9]), 'Wo': w(ks[10]), 'bo': b(ks[11])}
    _L3_gnn_all = _L3_gnn_setup()
    _L3_gnn_in = {k: v for k, v in _L3_gnn_all.items() if k in ('Wq', 'bq', 'Wk', 'bk', 'Wv', 'bv', 'Wo', 'bo')}
    del _L3_gnn_all
    return {'x': x, 'src': src, 'dst': dst, 'edge_attr_128': edge_attr_128, 'edge_attr_128_n2': edge_attr_128_n2, 'L0_gnn_W1': _L0_gnn_in['W1'], 'L0_gnn_a_src1': _L0_gnn_in['a_src1'], 'L0_gnn_a_dst1': _L0_gnn_in['a_dst1'], 'L0_gnn_b1': _L0_gnn_in['b1'], 'L0_gnn_W2': _L0_gnn_in['W2'], 'L0_gnn_a_src2': _L0_gnn_in['a_src2'], 'L0_gnn_a_dst2': _L0_gnn_in['a_dst2'], 'L0_gnn_b2': _L0_gnn_in['b2'], 'L1_gnn_W': _L1_gnn_in['W'], 'L1_gnn_b': _L1_gnn_in['b'], 'L2_gnn_coeffs_t': _L2_gnn_in['coeffs_t'], 'L2_gnn_lin_weight': _L2_gnn_in['lin_weight'], 'L2_gnn_lin_bias': _L2_gnn_in['lin_bias'], 'L2_gnn_att_src': _L2_gnn_in['att_src'], 'L2_gnn_att_dst': _L2_gnn_in['att_dst'], 'L3_gnn_Wq': _L3_gnn_in['Wq'], 'L3_gnn_bq': _L3_gnn_in['bq'], 'L3_gnn_Wk': _L3_gnn_in['Wk'], 'L3_gnn_bk': _L3_gnn_in['bk'], 'L3_gnn_Wv': _L3_gnn_in['Wv'], 'L3_gnn_bv': _L3_gnn_in['bv'], 'L3_gnn_Wo': _L3_gnn_in['Wo'], 'L3_gnn_bo': _L3_gnn_in['bo']}

def reference(x, src, dst, edge_attr_128, edge_attr_128_n2, L0_gnn_W1, L0_gnn_a_src1, L0_gnn_a_dst1, L0_gnn_b1, L0_gnn_W2, L0_gnn_a_src2, L0_gnn_a_dst2, L0_gnn_b2, L1_gnn_W, L1_gnn_b, L2_gnn_coeffs_t, L2_gnn_lin_weight, L2_gnn_lin_bias, L2_gnn_att_src, L2_gnn_att_dst, L3_gnn_Wq, L3_gnn_bq, L3_gnn_Wk, L3_gnn_bk, L3_gnn_Wv, L3_gnn_bv, L3_gnn_Wo, L3_gnn_bo):
    import jax
    import jax.numpy as jnp

    def _L0_gnn_ref(x, edge_index, W1, a_src1, a_dst1, b1, W2, a_src2, a_dst2, b2):
        import jax, jax.numpy as jnp
        import numpy as np
        N, F_IN, C_OUT, H = (6250, 128, 32, 4)
        ALPHA = 0.5
        SLOPE = 0.2

        def _gat_conv(x, W, a_src, a_dst, b, src, dst):
            n = x.shape[0]
            h = (x @ W).reshape(n, H, C_OUT)
            e_src = jnp.sum(h * a_src[None], -1)
            e_dst = jnp.sum(h * a_dst[None], -1)
            e = jax.nn.leaky_relu(e_src[src] + e_dst[dst], SLOPE)
            m = jax.ops.segment_max(e, dst, num_segments=n)
            ex = jnp.exp(e - m[dst])
            denom = jax.ops.segment_sum(ex, dst, num_segments=n)
            att = ex / denom[dst]
            msg = h[src] * att[:, :, None]
            out = jax.ops.segment_sum(msg, dst, num_segments=n)
            return out.reshape(n, H * C_OUT) + b
        n = x.shape[0]
        loops = jnp.arange(n, dtype=edge_index.dtype)
        src = jnp.concatenate([edge_index[0], loops])
        dst = jnp.concatenate([edge_index[1], loops])
        src_t = jnp.concatenate([edge_index[1], loops])
        dst_t = jnp.concatenate([edge_index[0], loops])
        out_fwd = _gat_conv(x, W1, a_src1, a_dst1, b1, src, dst)
        out_bwd = _gat_conv(x, W2, a_src2, a_dst2, b2, src_t, dst_t)
        return (1.0 - ALPHA) * out_fwd + ALPHA * out_bwd

    def _L1_gnn_ref(features, W, b, src, dst):
        import jax, jax.numpy as jnp
        import numpy as np
        EPS = 1e-12
        N = features.shape[0]
        neigh_sum = jax.ops.segment_sum(features[src], dst, num_segments=N)
        total = jnp.sum(features, axis=0)
        h_NN = total[None, :] - neigh_sum
        norm = jnp.sqrt(jnp.sum(h_NN * h_NN, axis=1, keepdims=True))
        h_norm = h_NN / jnp.maximum(norm, EPS)
        return h_norm @ W.T + b

    def _L2_gnn_ref(x, edge_index, coeffs_t, lin_weight, lin_bias, att_src, att_dst):
        import jax, jax.numpy as jnp
        import numpy as np
        N = 6250
        E = 75000
        IN = 128
        H = 4
        C = 32
        B = 3
        NEG_SLOPE = 0.2
        W = jnp.einsum('b,boi->oi', coeffs_t, lin_weight)
        bias = jnp.einsum('b,bo->o', coeffs_t, lin_bias)
        a_src = jnp.einsum('b,bqhc->qhc', coeffs_t, att_src)
        a_dst = jnp.einsum('b,bqhc->qhc', coeffs_t, att_dst)
        n = x.shape[0]
        xt = (x @ W.T + bias).reshape(n, H, C)
        alpha_src = jnp.sum(xt * a_src, axis=-1)
        alpha_dst = jnp.sum(xt * a_dst, axis=-1)
        row, col = (edge_index[0], edge_index[1])
        alpha = alpha_src[row] + alpha_dst[col]
        alpha = jax.nn.leaky_relu(alpha, NEG_SLOPE)
        amax = jax.ops.segment_max(alpha, col, num_segments=n)
        ex = jnp.exp(alpha - amax[col])
        denom = jax.ops.segment_sum(ex, col, num_segments=n)
        alpha = ex / (denom[col] + 1e-16)
        msg = xt[row] * alpha[..., None]
        out = jax.ops.segment_sum(msg, col, num_segments=n)
        return out.reshape(n, H * C)

    def _L3_gnn_ref(q_nodes, k_edges, v_edges, edge_index, Wq, bq, Wk, bk, Wv, bv, Wo, bo):
        import jax, jax.numpy as jnp
        import numpy as np
        DIM, HEADS = (128, 8)
        DH = DIM // HEADS
        SCALE = DH ** (-0.5)
        N, E = (6250, 100000)
        n, e = (q_nodes.shape[0], k_edges.shape[0])
        dst = edge_index[0]
        q = (q_nodes @ Wq.T + bq).reshape(n, HEADS, DH)
        k = (k_edges @ Wk.T + bk).reshape(e, HEADS, DH)
        v = (v_edges @ Wv.T + bv).reshape(e, HEADS, DH)
        score = jnp.einsum('ehd,ehd->eh', q[dst], k) * SCALE
        m = jax.ops.segment_max(score, dst, num_segments=n)
        ex = jnp.exp(score - m[dst])
        s = jax.ops.segment_sum(ex, dst, num_segments=n)
        w = ex / (s[dst] + 1e-16)
        weighted_v = (v * w[..., None]).reshape(e, DIM)
        aggr = jax.ops.segment_sum(weighted_v, dst, num_segments=n)
        return aggr @ Wo.T + bo
    edge_index = jnp.stack([src, dst])
    h = jnp.maximum(_layernorm(x, axis=-1), 0.0)
    x = x + _L0_gnn_ref(h, edge_index, L0_gnn_W1, L0_gnn_a_src1, L0_gnn_a_dst1, L0_gnn_b1, L0_gnn_W2, L0_gnn_a_src2, L0_gnn_a_dst2, L0_gnn_b2)
    h = jnp.maximum(_layernorm(x, axis=-1), 0.0)
    x = x + _L1_gnn_ref(h, L1_gnn_W, L1_gnn_b, src, dst)
    h = jnp.maximum(_layernorm(x, axis=-1), 0.0)
    x = x + _L2_gnn_ref(h, edge_index, L2_gnn_coeffs_t, L2_gnn_lin_weight, L2_gnn_lin_bias, L2_gnn_att_src, L2_gnn_att_dst)
    h = jnp.maximum(_layernorm(x, axis=-1), 0.0)
    x = x + _L3_gnn_ref(h, edge_attr_128, edge_attr_128_n2, edge_index, L3_gnn_Wq, L3_gnn_bq, L3_gnn_Wk, L3_gnn_bk, L3_gnn_Wv, L3_gnn_bv, L3_gnn_Wo, L3_gnn_bo)
    return x

_drawn_inputs = setup_inputs


def setup_inputs(seed=0):
    import zlib

    import numpy as np

    out = dict(_drawn_inputs(seed))
    spreads = {'L2_gnn_lin_bias': (0.0, 0.1)}
    factors = {'edge_attr_128': 8.0,
     'edge_attr_128_n2': 7.148,
     'L0_gnn_a_src1': 2.679,
     'L0_gnn_a_dst1': 7.63,
     'L0_gnn_a_dst2': 7.515,
     'L2_gnn_att_dst': 4.427,
     'L3_gnn_Wq': 8.0,
     'L3_gnn_bq': 8.0,
     'L3_gnn_Wk': 8.0,
     'L3_gnn_bk': 64.0,
     'L3_gnn_Wv': 7.25,
     'L3_gnn_bv': 27.465,
     'L3_gnn_Wo': 6.329,
     'L3_gnn_bo': 23.8}
    for name, (base, spread) in spreads.items():
        noise = np.random.default_rng([zlib.crc32(name.encode()), seed]).standard_normal(out[name].shape)
        drawn = base * np.exp(spread * noise) if base else spread * noise
        out[name] = jnp.asarray(drawn.astype(out[name].dtype))
    for name, factor in factors.items():
        out[name] = (out[name] * factor).astype(out[name].dtype)
    return out
```

```python
from contextlib import ExitStack

import concourse.bass as bass
from concourse import mybir

F32 = mybir.dt.float32
I32 = mybir.dt.int32
U32 = mybir.dt.uint32
BF16 = mybir.dt.bfloat16
ALU = mybir.AluOpType
ACT = mybir.ActivationFunctionType
AX = mybir.AxisListType

P = 128
N = 6250
E = 206250
D = 128
NB = -(-N // P)
NODES = NB * P
TAILN = N - (NB - 1) * P
G = 4
GE = G * P
NG = (E + NB * (GE - 1)) // GE
NG += NG % 2
SLOTS = NG * GE
CH = 9
TC = -(-E // P)
TC += -TC % (2 * CH)
NCHUNK = TC // CH
TAIL = E - (P - 1) * TC
BK = NB + 1
PADS = P * TC - E
FAR = 1.0e30


class Steps:

    def __init__(self, engine, sem):
        self.engine, self.sem, self.now, self.n = engine, sem, 0, 0

    def did(self, instruction):
        instruction.then_inc(self.sem, 1)
        self.n += 1

    def wait(self):
        self.engine.wait_ge(self.sem, self.now + self.n)

    def enter(self, i, per, first=0):
        self.before, self.per = self.now + self.n, per
        self.now, self.n = i * per + (self.before - first * per), 0

    def leave(self, passes):
        assert self.n == self.per, (self.n, self.per)
        self.now, self.n = self.before + passes * self.per, 0


class Phase(ExitStack):

    def __init__(self, nc):
        super().__init__()
        self.nc, self.sems, self.borrowed = nc, [], []

    def borrow(self, sems):
        self.sems += sems
        self.borrowed += sems
        return sems

    def __exit__(self, *raised):
        if self.sems and raised[0] is None:
            with self.nc.Block() as block:
                @block.gpsimd
                def _(pool):
                    for s in self.borrowed:
                        pool.dma_reset(range(s.num, s.num + 1))
                    for s in self.sems:
                        pool.sem_clear(s)
        return super().__exit__(*raised)


def memory(nc, ctx, tag=""):
    def sb(name, shape, dt=F32):
        return ctx.enter_context(nc.sbuf_tensor(tag + name, shape, dt))

    def pb(name, shape, dt=F32):
        return ctx.enter_context(nc.psum_tensor(tag + name, shape, dt))

    def sem(name):
        ctx.sems.append(ctx.enter_context(nc.semaphore(tag + name)))
        return ctx.sems[-1]
    return sb, pb, sem


def constants(nc, ctx):
    sb, pb, sem = memory(nc, ctx)
    c = {
        "ident": sb("ident", [P, P]), "ones": sb("ones", [P, P]), "zeros": sb("zeros", [P, 512]),
        "ones_h": sb("ones_h", [P, P], BF16), "below_h": sb("below_h", [P, P], BF16),
        "zeros_h": sb("zeros_h", [P, 512], BF16), "lanes": sb("lanes", [P, P]), "lanes_i": sb("lanes_i", [P, P], I32),
        "groups": sb("groups_n", [P, NG]), "groups_i": sb("groups_ni", [P, NG], I32),
        "headmask": sb("headmask", [P, 4]), "headmask3": sb("headmask3", [P, 8]),
    }
    c["indirect"] = [sem(f"indirect{n}") for n in range(4)]
    s_set, s_made = sem("const_set"), sem("const_made")
    with nc.Block() as block:
        @block.vector
        def _(dve):
            nc.vector.memset(c["ones"][:, :], 1.0)
            nc.vector.memset(c["zeros"][:, :], 0.0)
            nc.vector.memset(c["ones_h"][:, :], 1.0)
            nc.vector.memset(c["zeros_h"][:, :], 0.0)
            nc.vector.memset(c["headmask"][:, :], 0.0).then_inc(s_set, 1)
            dve.wait_ge(s_set, 1)
            for h in range(4):
                nc.vector.memset(c["headmask"][32 * h:32 * h + 32, h:h + 1], 1.0)
            dve.wait_ge(s_made, 2)
            nc.vector.tensor_copy(c["lanes"][:, :], c["lanes_i"][:, :])
            nc.vector.tensor_copy(c["groups"][:, :], c["groups_i"][:, :])

        @block.gpsimd
        def _(pool):
            nc.gpsimd.iota(c["lanes_i"][:, :], [[1, P]], base=0, channel_multiplier=0).then_inc(s_made, 1)
            nc.gpsimd.iota(c["groups_i"][:, :], [[1, NG]], base=0, channel_multiplier=0).then_inc(s_made, 1)
            nc.gpsimd.memset(c["ident"][:, :], 0.0).then_inc(s_made, 1)
            nc.gpsimd.memset(c["below_h"][:, :], 1.0).then_inc(s_made, 1)
            nc.gpsimd.memset(c["headmask3"][:, :], 1.0).then_inc(s_made, 1)
            pool.wait_ge(s_made, 5)
            nc.gpsimd.affine_select(out=c["ident"][:, :], in_=c["ident"][:, :], compare_op=ALU.not_equal, fill=1.0,
                                    base=0, pattern=[[-1, P]], channel_multiplier=1).then_inc(s_made, 1)
            nc.gpsimd.affine_select(out=c["below_h"][:, :], in_=c["below_h"][:, :], compare_op=ALU.is_gt, fill=0.0,
                                    base=0, pattern=[[1, P]], channel_multiplier=-1).then_inc(s_made, 1)
            nc.gpsimd.affine_select(out=c["headmask3"][:, :], in_=c["headmask3"][:, :], compare_op=ALU.is_ge, fill=0.0,
                                    base=0, pattern=[[-16, 8]], channel_multiplier=1).then_inc(s_made, 1)
            pool.wait_ge(s_made, 8)
            nc.gpsimd.affine_select(out=c["headmask3"][:, :], in_=c["headmask3"][:, :], compare_op=ALU.is_ge, fill=0.0,
                                    base=15, pattern=[[16, 8]], channel_multiplier=-1).then_inc(s_made, 1)
            pool.wait_ge(s_made, 9)
    return c


def bucket_edges(nc, const, tag, key, other, slots, group_block):
    with Phase(nc) as ctx:
        sb, pb, sem = memory(nc, ctx, tag)
        key_i = sb("key_i", [P, TC], I32)
        other_i = sb("other_i", [P, TC], I32)
        key_block = sb("key_block", [P, TC])
        pay = sb("pay", [P, TC, 4], I32)
        empty = sb("empty", [P, SLOTS // P, 4], I32)
        hot = sb("hot", [P, 2, CH, BK], BF16)
        count = sb("count", [P, BK])
        whole = sb("whole", [P, BK], I32)
        last = sb("last", [P, BK])
        run = sb("run", [P, BK])
        gb_f = sb("gb_f", [P, 2, NG])
        ranked = sb("ranked", [P, CH, BK])
        pos_f = sb("pos_f", [P, CH])
        pos = sb("pos", [P, 2, CH], U32)
        send = sb("send", [P, 2, CH, 4], I32)
        hist = pb("hist", [P, 512])
        pre = pb("pre", [P, 2, 512])

        s_load, s_pad, s_numbered, s_empty = sem("loaded"), sem("padded"), sem("numbered"), sem("emptied")
        s_step, s_hot, s_hist, s_hist_end = sem("vector_step"), sem("hot_ready"), sem("hist_added"), sem("hist_done")
        s_hot2, s_pre, s_used = sem("hot2_ready"), sem("prefix_ready"), sem("prefix_used")
        s_pos, s_past, s_init = sem("slots_ready"), sem("pool_past_wait"), sem("slots_emptied")
        s_scat = ctx.borrow(const["indirect"][0:2])
        HALF = NCHUNK // 2

        with nc.Block() as block:
            @block.sync
            def _(sp):
                sp.wait_ge(s_pad, 1)
                for a, t in ((key, key_i), (other, other_i)):
                    sp.dma_start(t[0:P - 1, :], a[0:(P - 1) * TC].rearrange("(p c) -> p c", p=P - 1)).then_inc(s_load, 16)
                    sp.dma_start(t[P - 1:P, 0:TAIL], a[(P - 1) * TC:E].rearrange("(p c) -> p c", p=1)).then_inc(s_load, 16)
                sp.wait_ge(s_empty, 1)
                sp.dma_start(slots[0:SLOTS, :].rearrange("(p s) f -> p (s f)", p=P),
                             empty[:, :, :].rearrange("p s f -> p (s f)")).then_inc(s_init, 16)

            @block.gpsimd
            def _(pool):
                nc.gpsimd.iota(pay[:, :, 2], [[1, TC]], base=0, channel_multiplier=TC).then_inc(s_numbered, 1)
                nc.gpsimd.iota(pay[:, :, 3], [[0, TC]], base=0, channel_multiplier=0).then_inc(s_numbered, 1)
                pool.wait_ge(s_init, 16)
                with pool.Fori(0, HALF) as i:
                    for h in range(2):
                        pool.wait_ge(s_pos, i * 4 + (2 * h + 2))
                        pool.sem_inc(s_past, 1)
                        for c in range(CH):
                            nc.gpsimd.indirect_dma_start(
                                slots[:, :], bass.IndirectOffsetOnAxis(ap=pos[:, h, c:c + 1], axis=0),
                                send[:, h, c, :], None).then_inc(s_scat[h], 16)
                for h in range(2):
                    pool.wait_ge(s_scat[h], 16 * CH * HALF)

            @block.tensor
            def _(pe):
                flat = hist[:, 0:CH * BK]
                pe.matmul(flat, const["ones_h"][:, :], const["zeros_h"][:, 0:CH * BK], start=True, stop=False)
                with pe.Fori(0, HALF) as i:
                    for h in range(2):
                        pe.wait_ge(s_hot, i * 2 + (h + 1))
                        pe.matmul(flat, const["ones_h"][:, :], hot[:, h, :, :].rearrange("p c b -> p (c b)"),
                                  start=False, stop=False).then_inc(s_hist, 1)
                pe.matmul(flat, const["ones_h"][:, :], const["zeros_h"][:, 0:CH * BK], start=False,
                          stop=True).then_inc(s_hist_end, 1)
                with pe.Fori(0, HALF) as i:
                    for h in range(2):
                        pe.wait_ge(s_hot2, i * 2 + (h + 1))
                        pe.wait_ge(s_used, i * 2 + (h + 1))
                        pe.matmul(pre[:, h, 0:(CH + 1) * BK], const["ones_h"][:, :],
                                  const["zeros_h"][:, 0:(CH + 1) * BK], start=True, stop=False)
                        for c in range(CH):
                            pe.matmul(pre[:, h, (c + 1) * BK:(CH + 1) * BK].rearrange("p (c b) -> p c b", b=BK),
                                      const["ones_h"][:, :], hot[:, h, c:c + 1, :].to_broadcast([P, CH - c, BK]),
                                      start=False, stop=False)
                        pe.matmul(pre[:, h, 0:CH * BK], const["below_h"][:, :],
                                  hot[:, h, :, :].rearrange("p c b -> p (c b)"), start=False, stop=True).then_inc(s_pre, 1)

            @block.vector
            def _(dve):
                st = Steps(dve, s_step)
                st.did(nc.vector.memset(key_i[:, :], NODES))
                st.did(nc.vector.memset(other_i[:, :], 0))
                st.wait()
                nc.vector.memset(empty[:, :, 0].bitcast(F32), -1.0).then_inc(s_pad, 1)
                nc.vector.memset(empty[:, :, 1], NODES - 1)
                nc.vector.memset(empty[:, :, 2:4], 0).then_inc(s_empty, 1)
                dve.wait_ge(s_load, 64)
                st.did(nc.vector.tensor_copy(pay[:, :, 1], other_i[:, :]))
                st.wait()
                st.did(nc.vector.tensor_scalar(other_i[:, :], key_i[:, :], P - 1, None, ALU.bitwise_and))
                st.did(nc.vector.tensor_scalar(key_i[:, :], key_i[:, :], 7, None, ALU.arith_shift_right))
                st.wait()
                st.did(nc.vector.tensor_copy(pay[:, :, 0].bitcast(F32), other_i[:, :]))
                st.did(nc.vector.tensor_copy(key_block[:, :], key_i[:, :]))
                st.wait()

                def one_hot(i, h):
                    return nc.vector.tensor_tensor(
                        hot[:, h, :, :], key_block[:, bass.ds(i * (2 * CH) + h * CH, CH)].unsqueeze(2).to_broadcast([P, CH, BK]),
                        const["lanes"][:, 0:BK].unsqueeze(1).to_broadcast([P, CH, BK]), ALU.is_equal)

                dve.sem_inc(s_hist, 2)
                with dve.Fori(0, HALF) as i:
                    for h in range(2):
                        dve.wait_ge(s_hist, i * 2 + (h + 1))
                        one_hot(i, h).then_inc(s_hot, 1)
                dve.wait_ge(s_hist_end, 1)
                st.did(nc.vector.tensor_reduce(count[:, :], hist[:, 0:CH * BK].rearrange("p (c b) -> p b c", b=BK), AX.X, ALU.add))
                st.wait()
                st.did(nc.vector.tensor_scalar(whole[:, :], count[:, :], float(GE - 1), None, ALU.add))
                st.wait()
                st.did(nc.vector.tensor_scalar(whole[:, :], whole[:, :], GE.bit_length() - 1, None, ALU.arith_shift_right))
                st.wait()
                st.did(nc.vector.tensor_copy(count[:, :], whole[:, :]))
                st.wait()
                st.did(nc.vector.tensor_tensor_scan(last[:, :], const["ones"][:, 0:BK], count[:, :], 0.0, ALU.mult, ALU.add))
                st.wait()
                st.did(nc.vector.tensor_tensor(run[:, :], last[:, :], count[:, :], ALU.subtract))
                st.wait()
                st.did(nc.vector.tensor_scalar(run[:, :], run[:, :], float(GE), None, ALU.mult))
                st.wait()
                st.did(nc.vector.memset(run[:, NB:BK], float(SLOTS)))
                st.did(nc.vector.memset(gb_f[:, 1, :], 0.0))
                for b in range(NB - 1):
                    st.wait()
                    st.did(nc.vector.scalar_tensor_tensor(gb_f[:, b % 2, :], const["groups"][:, :], last[:, b:b + 1],
                                                          gb_f[:, (b + 1) % 2, :], ALU.is_ge, ALU.add))
                st.wait()
                st.did(nc.vector.tensor_copy(group_block[:, :], gb_f[:, (NB - 2) % 2, :]))
                st.wait()
                dve.wait_ge(s_numbered, 2)
                dve.sem_inc(s_used, 2)

                def rank_chunk(i, h, ring_used):
                    one_hot(i, h).then_inc(s_hot2, 1)
                    dve.wait_ge(s_pre, i * 2 + (h + 1))
                    st.did(nc.vector.tensor_tensor(
                        ranked[:, :, :], pre[:, h, 0:CH * BK].rearrange("p (c b) -> p c b", b=BK),
                        run[:, :].unsqueeze(1).to_broadcast([P, CH, BK]), ALU.add))
                    st.wait()
                    nc.vector.tensor_tensor(run[:, :], run[:, :], pre[:, h, CH * BK:(CH + 1) * BK],
                                            ALU.add).then_inc(s_used, 1)
                    st.did(nc.vector.tensor_tensor(ranked[:, :, :], ranked[:, :, :], hot[:, h, :, :], ALU.mult))
                    st.wait()
                    st.did(nc.vector.tensor_reduce(pos_f[:, :], ranked[:, :, :], AX.X, ALU.add))
                    st.wait()
                    if ring_used:
                        dve.wait_ge(s_scat[h], i * (16 * CH))
                    nc.vector.tensor_copy(pos[:, h, :], pos_f[:, :]).then_inc(s_pos, 1)
                    nc.vector.tensor_copy(send[:, h, :, :],
                                          pay[:, bass.ds(i * (2 * CH) + h * CH, CH), :]).then_inc(s_pos, 1)
                    dve.wait_ge(s_used, i * 2 + (h + 3))
                    dve.wait_ge(s_pos, i * 4 + (2 * h + 2))

                for h in range(2):
                    rank_chunk(0, h, False)
                with dve.Fori(1, HALF) as i:
                    st.enter(i, 6, 1)
                    for h in range(2):
                        rank_chunk(i, h, True)
                    st.leave(HALF - 1)


H = 4
HC = D // H
ROW = D + H
TABW = ROW + H
U = 4


def at_pass(steps, k, per):
    steps.now, steps.n, steps.per = k * per, 0, per


def end_pass(steps):
    assert steps.n == steps.per, (steps.n, steps.per)


def groups_loop(engine, body):
    for r in range(U):
        body(r, r, True, False)
    with engine.Fori(1, NG // U - 1) as i:
        for r in range(U):
            body(i * U + r, r, False, False)
    for r in range(U):
        body(NG - U + r, r, False, True)


def gat_edges(nc, const, tag, slots, group_block, table, ed, shift, acc):
    AHEAD = 3
    with Phase(nc) as ctx:
        sb, pb, sem = memory(nc, ctx, tag)
        slot = sb("slot", [P, NG * G, 4], I32)
        idx = sb("idx", [P, U, G], U32)
        rows = sb("rows", [P, U, G, TABW])
        hot = sb("hot", [P, U, G, P])
        hot_t = sb("hot_t", [P, U, G * P])
        far = sb("far", [P, U, G * P])
        junk = sb("junk", [P, H, G * P], BF16)
        gmax = sb("gmax", [P, H])
        lin = sb("lin", [P, H])
        look = sb("look", [P, 2, 2 * H])
        drop = sb("drop", [P, 2, H])
        scale = sb("scale", [P, 2, H])
        za = sb("za", [P, G, H])
        zb = sb("zb", [P, G, H])
        zc = sb("zc", [P, G, H])
        w = sb("w", [P, G, H])
        hot_ps = pb("hot_ps", [P, 2, G * P])
        es_ps = pb("es_ps", [P, H, G * P])
        look_ps = pb("look_ps", [P, 2, G, 2 * H])
        sum_ps = pb("sum_ps", [P, ROW])

        s_slot, s_idx, s_past = sem("slots_loaded"), sem("idx_ready"), sem("pool_past_wait")
        s_dpast, s_shift_step = sem("vector_past_wait"), sem("shift_step")
        s_rows = ctx.borrow(const["indirect"])
        s_hot, s_hot_ps, s_hot_t, s_far = sem("hot"), sem("hot_turned"), sem("hot_t_copied"), sem("far_ready")
        s_es, s_max, s_shift, s_look = sem("es_spread"), sem("max_taken"), sem("shift_ready"), sem("looked_up")
        s_drop, s_scale, s_z, s_w = sem("drop_ready"), sem("scale_ready"), sem("z_ready"), sem("w_ready")
        s_msg, s_sum, s_add, s_step = sem("messages"), sem("summed"), sem("added"), sem("vector_step")

        with nc.Block() as block:
            @block.sync
            def _(sp):
                sp.dma_start(slot[:, :, :].rearrange("p (g j) f -> p g (j f)", j=G),
                             slots[0:SLOTS, :].rearrange("(g p j) f -> p g (j f)", p=P, j=G)).then_inc(s_slot, 16)
                sp.wait_ge(s_slot, 16)

            @block.gpsimd
            def _(pool):
                def gather(k, r, first, last):
                    pool.wait_ge(s_idx, k + 1)
                    if not first:
                        pool.wait_ge(s_sum, k + (1 - U))
                    pool.sem_inc(s_past, 1)
                    for j in range(G):
                        nc.gpsimd.indirect_dma_start(
                            rows[:, r, j, :], None, table[:, :],
                            bass.IndirectOffsetOnAxis(ap=idx[:, r, j:j + 1], axis=0)).then_inc(s_rows[r], 16)
                groups_loop(pool, gather)
                for r in range(U):
                    pool.wait_ge(s_rows[r], NG // U * 16 * G)

            @block.scalar
            def _(act):
                act.wait_ge(s_slot, 16)

                def index(k, r, wait=True):
                    if wait:
                        act.wait_ge(s_rows[r], (k - r) * (16 * G // U))
                    nc.scalar.copy(idx[:, r, :], slot[:, bass.ds(k * G, G), 1]).then_inc(s_idx, 1)

                def turned(k, r):
                    act.wait_ge(s_hot_ps, k + 1)
                    nc.scalar.copy(hot_t[:, r, :], hot_ps[:, r % 2, :]).then_inc(s_hot_t, 1)
                    nc.scalar.activation(far[:, r, :], hot_ps[:, r % 2, :], ACT.Copy, bias=-FAR,
                                         scale=FAR).then_inc(s_far, 1)

                def rescale(k, r):
                    act.wait_ge(s_drop, k + 1)
                    nc.scalar.activation(scale[:, r % 2, :], drop[:, r % 2, :], ACT.Exp).then_inc(s_scale, 1)

                def group(k, r, first, last):
                    if not last:
                        index(k + U, r)
                    act.wait_ge(s_z, k + 1)
                    nc.scalar.activation(w[:, :, :], zc[:, :, :], ACT.Exp).then_inc(s_w, 1)
                    if not (last and r == U - 1):
                        rescale(k + 1, (r + 1) % U)
                    if not (last and r > 0):
                        turned(k + AHEAD, (r + AHEAD) % U)
                for r in range(U):
                    index(r, r, False)
                for r in range(AHEAD):
                    turned(r, r)
                rescale(0, 0)
                groups_loop(act, group)

            @block.tensor
            def _(pe):
                def turn(k, r):
                    pe.wait_ge(s_hot, k + 1)
                    if not (isinstance(k, int) and k < 2):
                        pe.wait_ge(s_far, k - 1)
                    for j in range(G):
                        mm = pe.transpose(hot_ps[:, r % 2, j * P:(j + 1) * P], hot[:, r, j, :], const["ident"][:, :])
                    mm.then_inc(s_hot_ps, 1)

                def spread(k, r, free=True):
                    pe.wait_ge(s_rows[r], (k - r) * (16 * G // U) + 16 * G)
                    for h in range(H):
                        if free:
                            pe.wait_ge(s_max, k * H + (h + 1 - H))
                        for j in range(G):
                            mm = pe.transpose(es_ps[:, h, j * P:(j + 1) * P],
                                              rows[:, r, j, ROW + h:ROW + h + 1].to_broadcast([P, P]), const["ident"][:, :])
                        mm.then_inc(s_es, 1)

                def look_up(k, r):
                    pe.wait_ge(s_shift, k * 2 + 2)
                    pe.wait_ge(s_hot_t, k + 1)
                    for j in range(G):
                        mm = pe.matmul(look_ps[:, r % 2, j, :], hot_t[:, r, j * P:(j + 1) * P], look[:, r % 2, :],
                                       start=True, stop=True)
                    mm.then_inc(s_look, 1)

                def group(k, r, first, last):
                    if not (last and r >= U - 2):
                        spread(k + 2, (r + 2) % U)
                    pe.wait_ge(s_msg, k + 1)
                    for j in range(G):
                        mm = pe.matmul(sum_ps[:, :], hot[:, r, j, :], rows[:, r, j, 0:ROW],
                                       start=(j == 0), stop=(j == G - 1))
                    mm.then_inc(s_sum, 1)
                    if not (last and r == U - 1):
                        look_up(k + 1, (r + 1) % U)
                    if not (last and r > 0):
                        turn(k + AHEAD, (r + AHEAD) % U)
                for r in range(AHEAD):
                    turn(r, r)
                spread(0, 0, False)
                look_up(0, 0)
                spread(1, 1)
                groups_loop(pe, group)

            @block.vector
            def _(dve):
                st, sh = Steps(dve, s_step), Steps(dve, s_shift_step)
                dve.wait_ge(s_slot, 16)

                def one_hot(k, r):
                    nc.vector.tensor_tensor(
                        hot[:, r, :, :], const["lanes"][:, :].unsqueeze(1).to_broadcast([P, G, P]),
                        slot[:, bass.ds(k * G, G), 0].bitcast(F32).unsqueeze(2).to_broadcast([P, G, P]),
                        ALU.is_equal).then_inc(s_hot, 1)

                def maxima(k, r):
                    dve.wait_ge(s_far, k + 1)
                    for h in range(H):
                        dve.wait_ge(s_es, k * H + (h + 1))
                        dve.sem_inc(s_dpast, 1)
                        nc.vector.tensor_tensor_reduce(junk[:, h, :], es_ps[:, h, :], far[:, r, :], 1.0, -2 * FAR,
                                                       ALU.add, ALU.max, gmax[:, h:h + 1]).then_inc(s_max, 1)

                def new_shift(k, r):
                    at_pass(sh, k, 3)
                    b = dve.value_load(group_block[0:1, bass.ds(k, 1)], min_val=0, max_val=NB - 1)
                    ed_b = ed[:, bass.ds(b, 1), :].rearrange("p b h -> p (b h)")
                    shift_b = shift[:, bass.ds(b, 1), :].rearrange("p b h -> p (b h)")
                    nc.vector.tensor_copy(look[:, r % 2, 0:H], ed_b).then_inc(s_shift, 1)
                    dve.wait_ge(s_max, k * H + H)
                    sh.did(nc.vector.tensor_tensor(gmax[:, :], gmax[:, :], ed_b, ALU.add))
                    sh.wait()
                    sh.did(nc.vector.scalar_tensor_tensor(lin[:, :], gmax[:, :], 0.2, gmax[:, :], ALU.mult, ALU.max))
                    sh.wait()
                    nc.vector.tensor_tensor(look[:, r % 2, H:2 * H], lin[:, :], shift_b, ALU.max).then_inc(s_shift, 1)
                    dve.wait_ge(s_shift, k * 2 + 2)
                    nc.vector.tensor_tensor(drop[:, r % 2, :], shift_b, look[:, r % 2, H:2 * H],
                                            ALU.subtract).then_inc(s_drop, 1)
                    dve.wait_ge(s_drop, k + 1)
                    sh.did(nc.vector.tensor_scalar(shift_b, look[:, r % 2, H:2 * H], 1.0, None, ALU.mult))
                    sh.wait()
                    end_pass(sh)

                def logits(k, r):
                    at_pass(st, k, 2)
                    dve.wait_ge(s_look, k + 1)
                    st.did(nc.vector.tensor_tensor(za[:, :, :], look_ps[:, r % 2, :, 0:H], rows[:, r, :, ROW:TABW], ALU.add))
                    st.wait()
                    st.did(nc.vector.scalar_tensor_tensor(zb[:, :, :], za[:, :, :], 0.2, za[:, :, :], ALU.mult, ALU.max))
                    st.wait()
                    nc.vector.tensor_tensor(zc[:, :, :], zb[:, :, :], look_ps[:, r % 2, :, H:2 * H],
                                            ALU.subtract).then_inc(s_z, 1)
                    end_pass(st)

                def messages(k, r):
                    dve.wait_ge(s_w, k + 1)
                    m = rows[:, r, :, 0:ROW].rearrange("p j (h c) -> p j h c", h=H)
                    nc.vector.tensor_tensor(m, m, w[:, :, :].unsqueeze(3).to_broadcast([P, G, H, HC + 1]),
                                            ALU.mult).then_inc(s_msg, 1)

                def add(k, r):
                    b = dve.value_load(group_block[0:1, bass.ds(k, 1)], min_val=0, max_val=NB - 1)
                    dve.wait_ge(s_sum, k + 1)
                    dve.wait_ge(s_scale, k + 1)
                    acc_b = acc[:, bass.ds(b, 1), :].rearrange("p b (h c) -> p (b h) c", h=H)
                    nc.vector.tensor_tensor(acc_b, acc_b, scale[:, r % 2, :].unsqueeze(2).to_broadcast([P, H, HC + 1]),
                                            ALU.mult).then_inc(s_add, 1)
                    dve.wait_ge(s_add, k * 2 + 1)
                    nc.vector.tensor_tensor(acc_b, acc_b, sum_ps[:, :].rearrange("p (h c) -> p h c", h=H),
                                            ALU.add).then_inc(s_add, 1)
                    dve.wait_ge(s_add, k * 2 + 2)

                def group(k, r, first, last):
                    ahead = not (last and r == U - 1)
                    logits(k, r)
                    if not (first and r == 0):
                        add(k - 1, (r - 1) % U)
                    if ahead:
                        maxima(k + 1, (r + 1) % U)
                    messages(k, r)
                    if ahead:
                        new_shift(k + 1, (r + 1) % U)
                    if not (last and r > 0):
                        if not (first and r == 0):
                            dve.wait_ge(s_sum, k)
                        one_hot(k + AHEAD, (r + AHEAD) % U)
                for r in range(AHEAD):
                    one_hot(r, r)
                maxima(0, 0)
                new_shift(0, 0)
                groups_loop(dve, group)
                add(NG - 1, U - 1)


def root(nc, act, m, s_var, s_std):
    act.wait_ge(s_var, 1)
    nc.scalar.activation(m[:, 1, :], m[:, 0, :], ACT.Sqrt).then_inc(s_std, 1)


def normed(nc, dve, st, x, h, sq, m, s_var, s_std):
    wide = [P, NB, D]
    st.did(nc.vector.tensor_reduce(m[:, 0, :], x[:, :, :], AX.X, ALU.add))
    st.wait()
    st.did(nc.vector.tensor_scalar(m[:, 0, :], m[:, 0, :], 1.0 / D, None, ALU.mult))
    st.wait()
    st.did(nc.vector.tensor_tensor(h[:, :, :], x[:, :, :], m[:, 0, :].unsqueeze(2).to_broadcast(wide), ALU.subtract))
    st.wait()
    st.did(nc.vector.tensor_tensor(sq, h[:, :, :], h[:, :, :], ALU.mult))
    st.wait()
    st.did(nc.vector.tensor_reduce(m[:, 1, :], sq, AX.X, ALU.add))
    st.wait()
    nc.vector.tensor_scalar(m[:, 0, :], m[:, 1, :], 1.0 / D, 1e-5, ALU.mult, ALU.add).then_inc(s_var, 1)
    dve.wait_ge(s_std, 1)
    st.did(nc.vector.reciprocal(m[:, 1, :], m[:, 1, :]))
    st.wait()
    st.did(nc.vector.scalar_tensor_tensor(h[:, :, :], h[:, :, :], 0.0, m[:, 1, :].unsqueeze(2).to_broadcast(wide),
                                          ALU.max, ALU.mult))
    st.wait()


class Project:
    B = 7

    def __init__(self, nc, ctx, const, tag, h, weight, bias, width, per):
        sb, pb, sem = memory(nc, ctx, tag)
        self.nc, self.const, self.h, self.weight, self.bias, self.width, self.per = nc, const, h, weight, bias, width, per
        self.ht_ps = pb("ht_ps", [P, 2, 512])
        self.stage = sb("stage", [P, self.B, D])
        self.ht = sb("ht", [P, self.B, P])
        self.out_ps = pb("out_ps", [P, 3, 512])
        self.s_h, self.s_turned, self.s_copied = sem("h_ready"), sem("h_turned"), sem("ht_copied")
        self.s_staged = sem("h_staged")
        self.s_ready, self.s_taken = sem("product_ready"), sem("product_taken")

    def product(self, n):
        return self.out_ps[:, n // 3, (n % 3) * self.width:(n % 3 + 1) * self.width]

    def products(self, bank):
        n = min(3, self.B - 3 * bank)
        return self.out_ps[:, bank, 0:n * self.width].rearrange("p (n w) -> p n w", w=self.width), 3 * bank, n

    def tensor(self, pe):
        with pe.Fori(0, NB // self.B) as i:
            pe.wait_ge(self.s_staged, i + 1)
            for n in range(self.B):
                mm = pe.transpose(self.ht_ps[:, n // 4, (n % 4) * P:(n % 4 + 1) * P],
                                  self.stage[:, n, :],
                                  self.const["ident"][:, :])
            mm.then_inc(self.s_turned, 1)
            pe.wait_ge(self.s_copied, i * 2 + 2)
            pe.wait_ge(self.s_taken, i * self.per + self.per)
            for n in range(self.B):
                if self.bias is not None:
                    pe.matmul(self.product(n), self.const["ones"][0:1, :], self.bias, start=True, stop=False)
                mm = pe.matmul(self.product(n), self.ht[:, n, :], self.weight, start=self.bias is None, stop=True)
            mm.then_inc(self.s_ready, 1)

    def scalar(self, act):
        act.wait_ge(self.s_h, 1)
        with act.Fori(0, NB // self.B) as i:
            self.nc.scalar.copy(self.stage[:, :, :], self.h[:, bass.ds(i * self.B, self.B), :]).then_inc(self.s_staged, 1)
            act.wait_ge(self.s_turned, i + 1)
            self.nc.scalar.copy(self.ht[:, 0:4, :].rearrange("p n d -> p (n d)"), self.ht_ps[:, 0, :]).then_inc(self.s_copied, 1)
            self.nc.scalar.copy(self.ht[:, 4:7, :].rearrange("p n d -> p (n d)"), self.ht_ps[:, 1, 0:3 * P]).then_inc(self.s_copied, 1)

    def vector(self, dve, take):
        dve.sem_inc(self.s_taken, self.per)
        with dve.Fori(0, NB // self.B) as i:
            dve.wait_ge(self.s_ready, i + 1)
            take(i)
        dve.wait_ge(self.s_taken, self.per * (NB // self.B + 1))


WX = TABW + H


def gat_weights(nc, const, tag, w_in, a_src, a_dst, wx, bx, coeffs=None, bias=None):
    n = 1 if coeffs is None else coeffs.shape[0]
    with Phase(nc) as ctx:
        sb, pb, sem = memory(nc, ctx, tag)
        raw = sb("raw", [P, n, D])
        att = sb("att", [P, 2, n])
        mix = sb("mix", [P, n])
        mixed = sb("mixed", [P, 2, D])
        vec = sb("vec", [P, 2, 2])
        braw = sb("braw", [P, n])
        bcol = sb("bcol", [P, 2])
        turned = sb("turned", [P, D])
        heads = sb("heads", [P, 2 * H])
        turn_ps = pb("turn_ps", [P, D])
        att_ps = pb("att_ps", [P, 2 * H])
        b_ps = pb("b_ps", [1, D])
        ba_ps = pb("ba_ps", [1, 2 * H])
        s_in, s_v, s_t, s_pe = sem("loaded"), sem("vector_step"), sem("heads_ready"), sem("turned")
        s_c = sem("turned_copied")
        loads = 3 if coeffs is None else 8
        with nc.Block() as block:
            @block.sync
            def _(sp):
                if coeffs is None:
                    sp.dma_start(raw[:, 0, :], w_in).then_inc(s_in, 16)
                    for v, t in ((a_src, 0), (a_dst, 1)):
                        sp.dma_start(att[:, t, :], v.rearrange("h (c o) -> (h c) o", o=1)).then_inc(s_in, 16)
                else:
                    sp.dma_start(raw[:, :, :], w_in.rearrange("n o i -> o n i")).then_inc(s_in, 16)
                    sp.dma_start(mix[:, :], coeffs.rearrange("(o n) -> o n", o=1).to_broadcast([P, n])).then_inc(s_in, 16)
                    for m in range(n):
                        for v, t in ((a_src, 0), (a_dst, 1)):
                            sp.dma_start(att[:, t, m:m + 1], v[m, 0].rearrange("h (c o) -> (h c) o", o=1)).then_inc(s_in, 16)
                        sp.dma_start(braw[:, m:m + 1], bias[m].rearrange("(d o) -> d o", o=1)).then_inc(s_in, 16)

            @block.tensor
            def _(pe):
                pe.wait_ge(s_t, 1)
                raw_w = raw[:, 0, :] if coeffs is None else mixed[:, (n - 1) % 2, :]
                pe.transpose(turn_ps[:, :], raw_w, const["ident"][:, :]).then_inc(s_pe, 1)
                pe.wait_ge(s_c, 1)
                by_out = turned[:, :] if coeffs is None else raw_w
                pe.matmul(att_ps[:, :], by_out, heads[:, :], start=True, stop=True).then_inc(s_pe, 1)
                if coeffs is not None:
                    pe.matmul(b_ps[:, :], bcol[:, (n - 1) % 2:(n - 1) % 2 + 1], const["ident"][:, :], start=True, stop=True)
                    pe.matmul(ba_ps[:, :], bcol[:, (n - 1) % 2:(n - 1) % 2 + 1], heads[:, :], start=True, stop=True).then_inc(s_pe, 1)

            @block.vector
            def _(dve):
                st = Steps(dve, s_v)
                dve.wait_ge(s_in, 16 * (3 if coeffs is None else 2 + 3 * n))
                if coeffs is None:
                    srcs = [att[:, 0, 0:1], att[:, 1, 0:1]]
                else:
                    for m in range(n):
                        at, fr = m % 2, (m + 1) % 2
                        for dst, new, old in [(mixed[:, at, :], raw[:, m, :], mixed[:, fr, :]),
                                              (bcol[:, at:at + 1], braw[:, m:m + 1], bcol[:, fr:fr + 1]),
                                              (vec[:, 0, at:at + 1], att[:, 0, m:m + 1], vec[:, 0, fr:fr + 1]),
                                              (vec[:, 1, at:at + 1], att[:, 1, m:m + 1], vec[:, 1, fr:fr + 1])]:
                            if m == 0:
                                st.did(nc.vector.tensor_scalar(dst, new, mix[:, 0:1], None, ALU.mult))
                            else:
                                st.did(nc.vector.scalar_tensor_tensor(dst, new, mix[:, m:m + 1], old, ALU.mult, ALU.add))
                        st.wait()
                    at = (n - 1) % 2
                    srcs = [vec[:, 0, at:at + 1], vec[:, 1, at:at + 1]]
                for t in range(2):
                    st.did(nc.vector.tensor_scalar(heads[:, t * H:(t + 1) * H], const["headmask"][:, :], srcs[t], None, ALU.mult))
                st.did(nc.vector.memset(wx[:, :], 0.0))
                st.did(nc.vector.memset(bx[:, :], 0.0))
                st.wait()
                st.did(nc.vector.memset(bx[:, HC:ROW:HC + 1], 1.0))
                st.wait()
                dve.sem_inc(s_t, 1)
                dve.wait_ge(s_pe, 1)
                nc.vector.tensor_copy(turned[:, :], turn_ps[:, :]).then_inc(s_c, 1)
                cols = wx[:, 0:ROW].rearrange("p (h c) -> p h c", h=H)[:, :, 0:HC]
                by_in = raw[:, 0, :] if coeffs is None else turn_ps[:, :]
                st.did(nc.vector.tensor_copy(cols, by_in.rearrange("p (h c) -> p h c", h=H)))
                dve.wait_ge(s_pe, 2)
                st.did(nc.vector.tensor_copy(wx[:, ROW:WX], att_ps[:, :]))
                if coeffs is not None:
                    dve.wait_ge(s_pe, 3)
                    st.did(nc.vector.tensor_copy(bx[:, 0:ROW].rearrange("p (h c) -> p h c", h=H)[:, :, 0:HC],
                                                 b_ps[:, :].rearrange("p (h c) -> p h c", h=H)))
                    st.did(nc.vector.tensor_copy(bx[:, ROW:WX], ba_ps[:, :]))
                st.wait()


def gat_nodes(nc, const, tag, x, h, wx, bx, table, ed, shift, acc, loops):
    with Phase(nc) as ctx:
        sb, pb, sem = memory(nc, ctx, tag)
        rows = sb("rows", [P, NB, TABW])
        m = sb("moments", [P, 2, NB])
        lin = sb("lin", [P, NB, H])
        proj = Project(nc, ctx, const, tag + "proj", h, wx[:, :], bx[:, :], WX, 6)
        s_v, s_out = sem("vector_step"), sem("table_out")
        s_rows, s_var, s_std = sem("rows_ready"), sem("variance"), sem("deviation")
        with nc.Block() as block:
            @block.sync
            def _(sp):
                sp.wait_ge(s_rows, 1)
                sp.dma_start(table.rearrange("(b p) f -> p b f", p=P), rows[:, :, :]).then_inc(s_out, 16)
                sp.wait_ge(s_out, 16)

            @block.tensor
            def _(pe):
                proj.tensor(pe)

            @block.scalar
            def _(act):
                if x is not None:
                    root(nc, act, m, s_var, s_std)
                proj.scalar(act)

            @block.vector
            def _(dve):
                st = Steps(dve, s_v)
                if x is not None:
                    normed(nc, dve, st, x, h, acc[:, :, 0:D], m, s_var, s_std)
                dve.sem_inc(proj.s_h, 1)

                def take(i):
                    for bank in range(3):
                        ps, n0, n = proj.products(bank)
                        b = bass.ds(i * proj.B + n0, n)
                        nc.vector.tensor_scalar(rows[:, b, :], ps[:, :, 0:TABW], 1.0, None, ALU.mult).then_inc(proj.s_taken, 1)
                        nc.vector.tensor_copy(ed[:, b, :], ps[:, :, TABW:WX]).then_inc(proj.s_taken, 1)
                proj.vector(dve, take)
                dve.sem_inc(s_rows, 1)
                if loops:
                    st.did(nc.vector.tensor_copy(acc[:, :, :], rows[:, :, 0:ROW]))
                    st.did(nc.vector.tensor_tensor(lin[:, :, :], rows[:, :, ROW:TABW], ed[:, :, :], ALU.add))
                    st.wait()
                    st.did(nc.vector.scalar_tensor_tensor(shift[:, :, :], lin[:, :, :], 0.2, lin[:, :, :], ALU.mult, ALU.max))
                else:
                    st.did(nc.vector.memset(acc[:, :, :], 0.0))
                    st.did(nc.vector.memset(shift[:, :, :], -FAR))
                st.wait()


def gat_finish(nc, tag, x, acc, half, rows=()):
    with Phase(nc) as ctx:
        sb, pb, sem = memory(nc, ctx, tag)
        rec = sb("rec", [P, NB * H])
        add = sb("add", [P, D])
        s_in, s_v = sem("loaded"), sem("vector_step")
        with nc.Block() as block:
            @block.sync
            def _(sp):
                for row in rows:
                    sp.dma_start(add[:, :], row.rearrange("(o d) -> o d", o=1).to_broadcast([P, D])).then_inc(s_in, 16)

            @block.vector
            def _(dve):
                st = Steps(dve, s_v)
                a = acc[:, :, :].rearrange("p b (h c) -> p (b h) c", h=H)
                if half:
                    st.did(nc.vector.reciprocal(rec[:, :], a[:, :, HC]))
                    st.wait()
                    st.did(nc.vector.tensor_scalar(rec[:, :], rec[:, :], 0.5, None, ALU.mult))
                else:
                    st.did(nc.vector.tensor_scalar(rec[:, :], a[:, :, HC], 1e-16, None, ALU.add))
                    st.wait()
                    st.did(nc.vector.reciprocal(rec[:, :], rec[:, :]))
                st.wait()
                st.did(nc.vector.tensor_tensor(a[:, :, 0:HC], a[:, :, 0:HC],
                                               rec[:, :].unsqueeze(2).to_broadcast([P, NB * H, HC]), ALU.mult))
                st.wait()
                xv = x[:, :, :].rearrange("p b (h c) -> p (b h) c", h=H)
                st.did(nc.vector.tensor_tensor(xv, xv, a[:, :, 0:HC], ALU.add))
                st.wait()
                if rows:
                    dve.wait_ge(s_in, 16)
                    st.did(nc.vector.tensor_scalar(add[:, :], add[:, :], 0.5, None, ALU.mult))
                    st.wait()
                    st.did(nc.vector.tensor_tensor(x[:, :, :], x[:, :, :], add[:, :].unsqueeze(1).to_broadcast([P, NB, D]),
                                                   ALU.add))
                    st.wait()


def load_x(nc, a, x):
    with Phase(nc) as ctx:
        sb, pb, sem = memory(nc, ctx, "x_")
        s_in, s_pad = sem("loaded"), sem("padded")
        with nc.Block() as block:
            @block.vector
            def _(dve):
                nc.vector.memset(x[:, NB - 1, :], 0.0).then_inc(s_pad, 1)

            @block.sync
            def _(sp):
                sp.dma_start(x[:, 0:NB - 1, :], a[0:(NB - 1) * P, :].rearrange("(b p) d -> p b d", p=P)).then_inc(s_in, 16)
                sp.wait_ge(s_pad, 1)
                sp.dma_start(x[0:TAILN, NB - 1, :], a[(NB - 1) * P:N, :]).then_inc(s_in, 16)
                sp.wait_ge(s_in, 32)


def store_x(nc, out, x):
    with Phase(nc) as ctx:
        sb, pb, sem = memory(nc, ctx, "out_")
        s_out = sem("stored")
        with nc.Block() as block:
            @block.sync
            def _(sp):
                sp.dma_start(out[0:(NB - 1) * P, :].rearrange("(b p) d -> p b d", p=P), x[:, 0:NB - 1, :]).then_inc(s_out, 16)
                sp.dma_start(out[(NB - 1) * P:N, :], x[0:TAILN, NB - 1, :]).then_inc(s_out, 16)
                sp.wait_ge(s_out, 32)


def sum_edges(nc, const, tag, slots, group_block, table, acc):
    with Phase(nc) as ctx:
        sb, pb, sem = memory(nc, ctx, tag)
        slot = sb("slot", [P, NG * G, 4], I32)
        idx = sb("idx", [P, U, G], U32)
        rows = sb("rows", [P, U, G, D])
        hot = sb("hot", [P, U, G, P])
        sum_ps = pb("sum_ps", [P, U, 512])
        s_slot, s_idx, s_past = sem("slots_loaded"), sem("idx_ready"), sem("pool_past_wait")
        s_rows = ctx.borrow(const["indirect"])
        s_hot, s_sum, s_add = sem("hot"), sem("summed"), sem("added")

        with nc.Block() as block:
            @block.sync
            def _(sp):
                sp.dma_start(slot[:, :, :].rearrange("p (g j) f -> p g (j f)", j=G),
                             slots[0:SLOTS, :].rearrange("(g p j) f -> p g (j f)", p=P, j=G)).then_inc(s_slot, 16)
                sp.wait_ge(s_slot, 16)

            @block.gpsimd
            def _(pool):
                def gather(k, r, first, last):
                    pool.wait_ge(s_idx, k + 1)
                    if not first:
                        pool.wait_ge(s_sum, k + (1 - U))
                    pool.sem_inc(s_past, 1)
                    for j in range(G):
                        nc.gpsimd.indirect_dma_start(
                            rows[:, r, j, :], None, table[:, :],
                            bass.IndirectOffsetOnAxis(ap=idx[:, r, j:j + 1], axis=0)).then_inc(s_rows[r], 16)
                groups_loop(pool, gather)
                for r in range(U):
                    pool.wait_ge(s_rows[r], NG // U * 16 * G)

            @block.scalar
            def _(act):
                act.wait_ge(s_slot, 16)

                def index(k, r, first, last):
                    if not first:
                        act.wait_ge(s_rows[r], (k - r) * (16 * G // U))
                    nc.scalar.copy(idx[:, r, :], slot[:, bass.ds(k * G, G), 1]).then_inc(s_idx, 1)
                groups_loop(act, index)

            @block.tensor
            def _(pe):
                def add_up(k, r, first, last):
                    pe.wait_ge(s_rows[r], (k - r) * (16 * G // U) + 16 * G)
                    pe.wait_ge(s_hot, k + 1)
                    if not first:
                        pe.wait_ge(s_add, k + (1 - U))
                    for j in range(G):
                        mm = pe.matmul(sum_ps[:, r, 0:D], hot[:, r, j, :], rows[:, r, j, :],
                                       start=(j == 0), stop=(j == G - 1))
                    mm.then_inc(s_sum, 1)
                groups_loop(pe, add_up)

            @block.vector
            def _(dve):
                dve.wait_ge(s_slot, 16)

                def one_hot(k, r):
                    nc.vector.tensor_tensor(
                        hot[:, r, :, :], const["lanes"][:, :].unsqueeze(1).to_broadcast([P, G, P]),
                        slot[:, bass.ds(k * G, G), 0].bitcast(F32).unsqueeze(2).to_broadcast([P, G, P]),
                        ALU.is_equal).then_inc(s_hot, 1)

                def group(k, r, first, last):
                    b = dve.value_load(group_block[0:1, bass.ds(k, 1)], min_val=0, max_val=NB - 1)
                    if not (last and r >= 2):
                        if not (first and r < 2):
                            dve.wait_ge(s_sum, k + (3 - U))
                        one_hot(k + 2, (r + 2) % U)
                    acc_b = acc[:, bass.ds(b, 1), 0:D].rearrange("p b d -> p (b d)")
                    if not (first and r == 0):
                        dve.wait_ge(s_add, k)
                    dve.wait_ge(s_sum, k + 1)
                    nc.vector.tensor_tensor(acc_b, acc_b, sum_ps[:, r, 0:D], ALU.add).then_inc(s_add, 1)
                for r in range(2):
                    one_hot(r, r)
                groups_loop(dve, group)


def turned_weights(nc, const, tag, pairs):
    with Phase(nc) as ctx:
        sb, pb, sem = memory(nc, ctx, tag)
        raw = sb("raw", [P, len(pairs), D])
        ps = pb("ps", [P, 4, P])
        assert len(pairs) <= 4
        s_in, s_pe = sem("loaded"), sem("turned")
        with nc.Block() as block:
            @block.sync
            def _(sp):
                for n, (w, t) in enumerate(pairs):
                    sp.dma_start(raw[:, n, :], w).then_inc(s_in, 16)

            @block.tensor
            def _(pe):
                pe.wait_ge(s_in, 16 * len(pairs))
                for n in range(len(pairs)):
                    pe.transpose(ps[:, n, :], raw[:, n, :], const["ident"][:, :]).then_inc(s_pe, 1)

            @block.vector
            def _(dve):
                dve.wait_ge(s_pe, len(pairs))
                for n, (w, t) in enumerate(pairs):
                    nc.vector.tensor_copy(t, ps[:, n, :])


def complement_nodes(nc, tag, x, h, table, acc, const, total):
    with Phase(nc) as ctx:
        sb, pb, sem = memory(nc, ctx, tag)
        m = sb("moments", [P, 2, NB])
        ps = pb("ps", [P, D])
        s_v, s_out, s_h, s_pe = sem("vector_step"), sem("table_out"), sem("h_ready"), sem("total_ready")
        s_var, s_std = sem("variance"), sem("deviation")
        with nc.Block() as block:
            @block.sync
            def _(sp):
                sp.wait_ge(s_h, 1)
                sp.dma_start(table.rearrange("(b p) f -> p b f", p=P), h[:, :, :]).then_inc(s_out, 16)
                sp.wait_ge(s_out, 16)

            @block.scalar
            def _(act):
                root(nc, act, m, s_var, s_std)

            @block.tensor
            def _(pe):
                pe.wait_ge(s_h, 1)
                pe.matmul(ps[:, :], const["ones"][:, :], h[:, 0, :], start=True, stop=False)
                with pe.Fori(0, (NB - 3) // 2) as i:
                    for n in range(2):
                        pe.matmul(ps[:, :], const["ones"][:, :], h[:, bass.ds(i * 2 + (n + 1), 1), :].rearrange("p b d -> p (b d)"),
                                  start=False, stop=False)
                pe.matmul(ps[:, :], const["ones"][:, :], h[:, NB - 2, :], start=False, stop=False)
                pe.matmul(ps[:, :], const["ones"][0:TAILN, :], h[0:TAILN, NB - 1, :], start=False, stop=True).then_inc(s_pe, 1)

            @block.vector
            def _(dve):
                st = Steps(dve, s_v)
                normed(nc, dve, st, x, h, acc[:, :, 0:D], m, s_var, s_std)
                dve.sem_inc(s_h, 1)
                st.did(nc.vector.memset(acc[:, :, :], 0.0))
                dve.wait_ge(s_pe, 1)
                st.did(nc.vector.tensor_copy(total[:, :], ps[:, :]))
                st.wait()


def into_x(nc, proj, dve, x):
    def take(i):
        for bank in range(3):
            ps, n0, n = proj.products(bank)
            xb = x[:, bass.ds(i * proj.B + n0, n), :]
            nc.vector.tensor_tensor(xb, xb, ps, ALU.add).then_inc(proj.s_taken, 1)
    proj.vector(dve, take)


def complement_finish(nc, const, tag, x, h, acc, total, weight, bias):
    with Phase(nc) as ctx:
        sb, pb, sem = memory(nc, ctx, tag)
        n2 = sb("norm", [P, 2, NB])
        row = sb("row", [1, D])
        proj = Project(nc, ctx, const, tag + "proj", h, weight[:, :], row[:, :], D, 3)
        s_v, s_in, s_sq, s_root = sem("vector_step"), sem("loaded"), sem("squares"), sem("roots")
        with nc.Block() as block:
            @block.sync
            def _(sp):
                sp.dma_start(row[:, :], bias.rearrange("(o d) -> o d", o=1)).then_inc(s_in, 16)

            @block.tensor
            def _(pe):
                pe.wait_ge(s_in, 16)
                proj.tensor(pe)

            @block.scalar
            def _(act):
                act.wait_ge(s_sq, 1)
                nc.scalar.activation(n2[:, 1, :], n2[:, 0, :], ACT.Sqrt).then_inc(s_root, 1)
                proj.scalar(act)

            @block.vector
            def _(dve):
                st = Steps(dve, s_v)
                wide = [P, NB, D]
                sq = acc[:, :, 0:D]
                st.did(nc.vector.tensor_tensor(h[:, :, :], total[:, :].unsqueeze(1).to_broadcast(wide), acc[:, :, 0:D], ALU.subtract))
                st.wait()
                st.did(nc.vector.tensor_tensor(sq, h[:, :, :], h[:, :, :], ALU.mult))
                st.wait()
                nc.vector.tensor_reduce(n2[:, 0, :], sq, AX.X, ALU.add).then_inc(s_sq, 1)
                dve.wait_ge(s_root, 1)
                st.did(nc.vector.tensor_scalar(n2[:, 1, :], n2[:, 1, :], 1e-12, None, ALU.max))
                st.wait()
                st.did(nc.vector.reciprocal(n2[:, 1, :], n2[:, 1, :]))
                st.wait()
                st.did(nc.vector.tensor_tensor(h[:, :, :], h[:, :, :], n2[:, 1, :].unsqueeze(2).to_broadcast(wide), ALU.mult))
                st.wait()
                dve.sem_inc(proj.s_h, 1)
                into_x(nc, proj, dve, x)


H3 = 8
HC3 = D // H3
ROW3 = D + H3
QW = D + H3


def query_weights(nc, const, tag, wq, bq, bk, qx, qb):
    with Phase(nc) as ctx:
        sb, pb, sem = memory(nc, ctx, tag)
        raw = sb("raw", [P, D])
        cols = sb("cols", [P, 2])
        heads = sb("heads", [P, H3])
        ps = pb("ps", [P, D])
        ps_h = pb("ps_h", [P, H3])
        ps_b = pb("ps_b", [1, D + H3])
        s_in, s_v, s_t, s_pe = sem("loaded"), sem("vector_step"), sem("scaled"), sem("products")
        with nc.Block() as block:
            @block.sync
            def _(sp):
                sp.dma_start(raw[:, :], wq).then_inc(s_in, 16)
                sp.dma_start(cols[:, 0:1], bq.rearrange("(d o) -> d o", o=1)).then_inc(s_in, 16)
                sp.dma_start(cols[:, 1:2], bk.rearrange("(d o) -> d o", o=1)).then_inc(s_in, 16)

            @block.tensor
            def _(pe):
                pe.wait_ge(s_t, 3)
                pe.transpose(ps[:, :], raw[:, :], const["ident"][:, :])
                pe.matmul(ps_h[:, :], raw[:, :], heads[:, :], start=True, stop=True)
                pe.matmul(ps_b[:, 0:D], cols[:, 0:1], const["ident"][:, :], start=True, stop=True)
                pe.matmul(ps_b[:, D:QW], cols[:, 0:1], heads[:, :], start=True, stop=True).then_inc(s_pe, 1)

            @block.vector
            def _(dve):
                dve.wait_ge(s_in, 48)
                scale = float(HC3) ** -0.5
                nc.vector.tensor_scalar(heads[:, :], const["headmask3"][:, :], cols[:, 1:2], None, ALU.mult).then_inc(s_t, 1)
                nc.vector.tensor_scalar(raw[:, :], raw[:, :], scale, None, ALU.mult).then_inc(s_t, 1)
                nc.vector.tensor_scalar(cols[:, 0:1], cols[:, 0:1], scale, None, ALU.mult).then_inc(s_t, 1)
                dve.wait_ge(s_pe, 1)
                nc.vector.tensor_copy(qx[:, 0:D], ps[:, :]).then_inc(s_v, 1)
                nc.vector.tensor_copy(qx[:, D:QW], ps_h[:, :]).then_inc(s_v, 1)
                nc.vector.tensor_copy(qb[:, :], ps_b[:, :]).then_inc(s_v, 1)
                dve.wait_ge(s_v, 3)


def attention_nodes(nc, const, tag, x, h, qx, qb, queries, shift, acc):
    with Phase(nc) as ctx:
        sb, pb, sem = memory(nc, ctx, tag)
        m = sb("moments", [P, 2, NB])
        proj = Project(nc, ctx, const, tag + "proj", h, qx[:, :], qb[:, :], QW, 3)
        s_v, s_var, s_std = sem("vector_step"), sem("variance"), sem("deviation")
        with nc.Block() as block:
            @block.tensor
            def _(pe):
                proj.tensor(pe)

            @block.scalar
            def _(act):
                root(nc, act, m, s_var, s_std)
                proj.scalar(act)

            @block.vector
            def _(dve):
                st = Steps(dve, s_v)
                normed(nc, dve, st, x, h, acc[:, :, 0:D], m, s_var, s_std)
                dve.sem_inc(proj.s_h, 1)

                def take(i):
                    for bank in range(3):
                        ps, n0, n = proj.products(bank)
                        nc.vector.tensor_scalar(queries[:, bass.ds(i * proj.B + n0, n), :], ps, 1.0, None,
                                                ALU.mult).then_inc(proj.s_taken, 1)
                proj.vector(dve, take)
                st.did(nc.vector.memset(acc[:, :, :], 0.0))
                st.did(nc.vector.memset(shift[:, :, :], -FAR))
                st.wait()


def attention_edges(nc, const, tag, slots, group_block, keys, values, wk, wv, queries, shift, acc):
    with Phase(nc) as ctx:
        sb, pb, sem = memory(nc, ctx, tag)
        RU = 2
        slot = sb("slot", [P, NG * G, 4], I32)
        idx = sb("idx", [P, U, G], U32)
        krow = sb("krow", [P, RU, G, D])
        vrow = sb("vrow", [P, RU, G, D])
        hot = sb("hot", [P, 2, G, P])
        hot_t = sb("hot_t", [P, 2, G * P])
        far = sb("far", [P, 2, G * P])
        krow_t = sb("krow_t", [P, G * P])
        vrow_t = sb("vrow_t", [P, G * P])
        key = sb("key", [P, G * D])
        value = sb("value", [P, 2, G * H3, HC3 + 1])
        prod = sb("prod", [P, G * D])
        part = sb("part", [P, G * H3])
        score = sb("score", [P, 2, G, H3])
        junk = sb("junk", [P, 2, G * P], BF16)
        query = sb("query", [P, 2, QW])
        gmax = sb("gmax", [P, H3])
        new = sb("new", [P, 2, H3])
        drop = sb("drop", [P, 2, H3])
        scale = sb("scale", [P, 2, H3])
        z = sb("z", [P, G, H3])
        w = sb("w", [P, G * H3])
        msg = sb("msg", [P, G * H3, HC3 + 1])
        hot_ps = pb("hot_ps", [P, G * P])
        row_ps = pb("row_ps", [P, G * P])
        key_ps = pb("key_ps", [P, G * D])
        value_ps = pb("value_ps", [P, G * D])
        query_ps = pb("query_ps", [P, G * D])
        spread_ps = pb("spread_ps", [P, 2, G * P])
        misc_ps = pb("misc_ps", [P, 512])
        bias_ps = misc_ps[:, 0:G * H3].rearrange("p (j h) -> p j h", j=G)
        new_ps = misc_ps[:, G * H3:2 * G * H3].rearrange("p (j h) -> p j h", j=G)
        sum_ps = misc_ps[:, 128:128 + ROW3]

        s_slot, s_idx, s_past = sem("slots_loaded"), sem("idx_ready"), sem("pool_past_wait")
        s_krow, s_vrow = ctx.borrow(const["indirect"][0:RU]), ctx.borrow(const["indirect"][RU:2 * RU])
        s_hot, s_hot_ps, s_hot_t, s_far = sem("hot"), sem("hot_turned"), sem("hot_t_copied"), sem("far_ready")
        s_row_ps, s_row_t, s_key_ps, s_key = sem("row_turned"), sem("row_t_copied"), sem("key_product"), sem("key_copied")
        s_value_ps, s_value, s_ones = sem("value_product"), sem("value_copied"), sem("ones_set")
        s_query, s_query_ps, s_prod, s_score = sem("query_copied"), sem("queries_looked_up"), sem("product_taken"), sem("score_ready")
        s_spread, s_max, s_new, s_new_ps = sem("score_spread"), sem("max_taken"), sem("shift_ready"), sem("shift_looked_up")
        s_drop, s_scale, s_z, s_w = sem("drop_ready"), sem("scale_ready"), sem("z_ready"), sem("w_ready")
        s_msg, s_sum, s_add, s_step, s_dpast = sem("messages"), sem("summed"), sem("added"), sem("vector_step"), sem("vector_past_wait")

        with nc.Block() as block:
            @block.sync
            def _(sp):
                sp.dma_start(slot[:, :, :].rearrange("p (g j) f -> p g (j f)", j=G),
                             slots[0:SLOTS, :].rearrange("(g p j) f -> p g (j f)", p=P, j=G)).then_inc(s_slot, 16)
                sp.wait_ge(s_slot, 16)

            @block.gpsimd
            def _(pool):
                def gather(k, r, first, last):
                    pool.wait_ge(s_idx, k + 1)
                    if not (first and r < RU):
                        pool.wait_ge(s_row_ps, k * 2 + 2 * (1 - RU))
                    pool.sem_inc(s_past, 1)
                    for t, ring, s in ((keys, krow, s_krow), (values, vrow, s_vrow)):
                        for j in range(G):
                            nc.gpsimd.indirect_dma_start(
                                ring[:, r % RU, j, :], None, t[:, :],
                                bass.IndirectOffsetOnAxis(ap=idx[:, r, j:j + 1], axis=0)).then_inc(s[r % RU], 16)
                groups_loop(pool, gather)
                for r in range(RU):
                    pool.wait_ge(s_krow[r], NG // RU * 16 * G)
                    pool.wait_ge(s_vrow[r], NG // RU * 16 * G)

            @block.scalar
            def _(act):
                act.wait_ge(s_slot, 16)

                def index(k, r, wait=True):
                    if wait:
                        act.wait_ge(s_vrow[r % RU], (k - r) * (16 * G // RU) + (r // RU - U // RU + 1) * 16 * G)
                    nc.scalar.copy(idx[:, r, :], slot[:, bass.ds(k * G, G), 2]).then_inc(s_idx, 1)

                def rows(k, r):
                    act.wait_ge(s_row_ps, k * 2 + 1)
                    nc.scalar.copy(krow_t[:, :], row_ps[:, :]).then_inc(s_row_t, 1)
                    act.wait_ge(s_row_ps, k * 2 + 2)
                    nc.scalar.copy(vrow_t[:, :], row_ps[:, :]).then_inc(s_row_t, 1)
                    act.wait_ge(s_key_ps, k + 1)
                    nc.scalar.copy(key[:, :], key_ps[:, :]).then_inc(s_key, 1)
                    act.wait_ge(s_value_ps, k + 1)
                    nc.scalar.copy(value[:, r % 2, :, 0:HC3], value_ps[:, :].rearrange("p (x c) -> p x c", c=HC3)).then_inc(s_value, 1)

                def turned(k, r):
                    act.wait_ge(s_hot_ps, k + 1)
                    nc.scalar.copy(hot_t[:, r % 2, :], hot_ps[:, :]).then_inc(s_hot_t, 1)

                def distance(k, r):
                    nc.scalar.activation(far[:, r % 2, :], hot_ps[:, :], ACT.Copy, bias=-FAR, scale=FAR).then_inc(s_far, 1)

                def group(k, r, first, last):
                    ahead = not (last and r == U - 1)
                    if ahead:
                        rows(k + 1, (r + 1) % U)
                    act.wait_ge(s_drop, k + 1)
                    nc.scalar.activation(scale[:, r % 2, :], drop[:, r % 2, :], ACT.Exp).then_inc(s_scale, 1)
                    if ahead:
                        turned(k + 1, (r + 1) % U)
                    act.wait_ge(s_z, k + 1)
                    nc.scalar.activation(w[:, :], z[:, :, :].rearrange("p j h -> p (j h)"), ACT.Exp).then_inc(s_w, 1)
                    if ahead:
                        distance(k + 1, (r + 1) % U)
                    if not (last and r > 0):
                        index(k + U - 1, (r + U - 1) % U, not (first and r == 0))
                for r in range(U - 1):
                    index(r, r, False)
                rows(0, 0)
                turned(0, 0)
                distance(0, 0)
                groups_loop(act, group)

            @block.tensor
            def _(pe):
                def rows(k, r):
                    if not (isinstance(k, int) and k == 0):
                        pe.wait_ge(s_row_t, k * 2)
                    pe.wait_ge(s_krow[r % RU], (k - r) * (16 * G // RU) + (r // RU + 1) * 16 * G)
                    for j in range(G):
                        mm = pe.transpose(row_ps[:, j * P:(j + 1) * P], krow[:, r % RU, j, :], const["ident"][:, :])
                    mm.then_inc(s_row_ps, 1)
                    pe.wait_ge(s_row_t, k * 2 + 1)
                    pe.wait_ge(s_vrow[r % RU], (k - r) * (16 * G // RU) + (r // RU + 1) * 16 * G)
                    for j in range(G):
                        mm = pe.transpose(row_ps[:, j * P:(j + 1) * P], vrow[:, r % RU, j, :], const["ident"][:, :])
                    mm.then_inc(s_row_ps, 1)
                    if not (isinstance(k, int) and k == 0):
                        pe.wait_ge(s_value, k)
                    for j in range(G):
                        mm = pe.matmul(key_ps[:, j * D:(j + 1) * D], krow_t[:, j * P:(j + 1) * P], wk[:, :], start=True, stop=True)
                    mm.then_inc(s_key_ps, 1)
                    pe.wait_ge(s_row_t, k * 2 + 2)
                    for j in range(G):
                        mm = pe.matmul(value_ps[:, j * D:(j + 1) * D], vrow_t[:, j * P:(j + 1) * P], wv[:, :], start=True, stop=True)
                    mm.then_inc(s_value_ps, 1)

                def turn(k, r):
                    pe.wait_ge(s_hot, k + 1)
                    for j in range(G):
                        mm = pe.transpose(hot_ps[:, j * P:(j + 1) * P], hot[:, r % 2, j, :], const["ident"][:, :])
                    mm.then_inc(s_hot_ps, 1)

                def ask(k, r):
                    pe.wait_ge(s_hot_t, k + 1)
                    pe.wait_ge(s_query, k + 1)
                    if not (isinstance(k, int) and k == 0):
                        pe.wait_ge(s_z, k)
                    for j in range(G):
                        pe.matmul(query_ps[:, j * D:(j + 1) * D], hot_t[:, r % 2, j * P:(j + 1) * P], query[:, r % 2, 0:D],
                                  start=True, stop=True)
                        mm = pe.matmul(bias_ps[:, j, :], hot_t[:, r % 2, j * P:(j + 1) * P], query[:, r % 2, D:QW],
                                       start=True, stop=True)
                    mm.then_inc(s_query_ps, 1)

                def group(k, r, first, last):
                    ahead = not (last and r == U - 1)
                    pe.wait_ge(s_score, k + 1)
                    for h in range(H3):
                        if not (first and r == 0 and h < 2):
                            pe.wait_ge(s_max, k * H3 + (h - 1))
                        for j in range(G):
                            mm = pe.transpose(spread_ps[:, h % 2, j * P:(j + 1) * P],
                                              score[:, r % 2, j, h:h + 1].to_broadcast([P, P]), const["ident"][:, :])
                        mm.then_inc(s_spread, 1)
                    if ahead:
                        rows(k + 1, (r + 1) % U)
                    pe.wait_ge(s_new, k + 1)
                    if not (first and r == 0):
                        pe.wait_ge(s_add, k * 2)
                    for j in range(G):
                        mm = pe.matmul(new_ps[:, j, :], hot_t[:, r % 2, j * P:(j + 1) * P], new[:, r % 2, :], start=True, stop=True)
                    mm.then_inc(s_new_ps, 1)
                    if ahead:
                        turn(k + 1, (r + 1) % U)
                        ask(k + 1, (r + 1) % U)
                    pe.wait_ge(s_msg, k + 1)
                    for j in range(G):
                        mm = pe.matmul(sum_ps, hot[:, r % 2, j, :], msg[:, j * H3:(j + 1) * H3, :].rearrange("p h c -> p (h c)"),
                                       start=(j == 0), stop=(j == G - 1))
                    mm.then_inc(s_sum, 1)
                rows(0, 0)
                turn(0, 0)
                ask(0, 0)
                groups_loop(pe, group)

            @block.vector
            def _(dve):
                st = Steps(dve, s_step)
                nc.vector.memset(value[:, :, :, HC3], 1.0).then_inc(s_ones, 1)
                dve.wait_ge(s_ones, 1)
                dve.wait_ge(s_slot, 16)

                def one_hot(k, r):
                    nc.vector.tensor_tensor(
                        hot[:, r % 2, :, :], const["lanes"][:, :].unsqueeze(1).to_broadcast([P, G, P]),
                        slot[:, bass.ds(k * G, G), 0].bitcast(F32).unsqueeze(2).to_broadcast([P, G, P]),
                        ALU.is_equal).then_inc(s_hot, 1)
                    b = dve.value_load(group_block[0:1, bass.ds(k, 1)], min_val=0, max_val=NB - 1)
                    nc.vector.tensor_copy(query[:, r % 2, :], queries[:, bass.ds(b, 1), :].rearrange("p b q -> p (b q)")).then_inc(s_query, 1)

                def scores(k, r):
                    dve.wait_ge(s_query_ps, k + 1)
                    dve.wait_ge(s_key, k + 1)
                    nc.vector.tensor_tensor(prod[:, :], query_ps[:, :], key[:, :], ALU.mult).then_inc(s_prod, 1)
                    dve.wait_ge(s_prod, k * 2 + 1)
                    nc.vector.tensor_reduce(part[:, :], prod[:, :].rearrange("p (x c) -> p x c", c=HC3), AX.X, ALU.add).then_inc(s_prod, 1)
                    dve.wait_ge(s_prod, k * 2 + 2)
                    nc.vector.tensor_tensor(score[:, r % 2, :, :], part[:, :].rearrange("p (j h) -> p j h", j=G), bias_ps,
                                            ALU.add).then_inc(s_score, 1)

                def new_shift(k, r):
                    b = dve.value_load(group_block[0:1, bass.ds(k, 1)], min_val=0, max_val=NB - 1)
                    shift_b = shift[:, bass.ds(b, 1), :].rearrange("p b h -> p (b h)")
                    dve.wait_ge(s_far, k + 1)
                    for h in range(H3):
                        dve.wait_ge(s_spread, k * H3 + (h + 1))
                        dve.sem_inc(s_dpast, 1)
                        nc.vector.tensor_tensor_reduce(junk[:, h % 2, :], spread_ps[:, h % 2, :], far[:, r % 2, :], 1.0, -2 * FAR,
                                                       ALU.add, ALU.max, gmax[:, h:h + 1]).then_inc(s_max, 1)
                    dve.wait_ge(s_max, k * H3 + H3)
                    nc.vector.tensor_tensor(new[:, r % 2, :], gmax[:, :], shift_b, ALU.max).then_inc(s_new, 1)
                    dve.wait_ge(s_new, k + 1)
                    nc.vector.tensor_tensor(drop[:, r % 2, :], shift_b, new[:, r % 2, :], ALU.subtract).then_inc(s_drop, 1)
                    dve.wait_ge(s_drop, k + 1)
                    st.did(nc.vector.tensor_scalar(shift_b, new[:, r % 2, :], 1.0, None, ALU.mult))

                def logits(k, r):
                    st.wait()
                    dve.wait_ge(s_new_ps, k + 1)
                    nc.vector.tensor_tensor(z[:, :, :], score[:, r % 2, :, :], new_ps, ALU.subtract).then_inc(s_z, 1)

                def messages(k, r):
                    dve.wait_ge(s_value, k + 1)
                    dve.wait_ge(s_w, k + 1)
                    nc.vector.tensor_tensor(msg[:, :, :], value[:, r % 2, :, :],
                                            w[:, :].unsqueeze(2).to_broadcast([P, G * H3, HC3 + 1]), ALU.mult).then_inc(s_msg, 1)

                def add(k, r):
                    b = dve.value_load(group_block[0:1, bass.ds(k, 1)], min_val=0, max_val=NB - 1)
                    dve.wait_ge(s_sum, k + 1)
                    dve.wait_ge(s_scale, k + 1)
                    acc_b = acc[:, bass.ds(b, 1), :].rearrange("p b (h c) -> p (b h) c", h=H3)
                    nc.vector.tensor_tensor(acc_b, acc_b, scale[:, r % 2, :].unsqueeze(2).to_broadcast([P, H3, HC3 + 1]),
                                            ALU.mult).then_inc(s_add, 1)
                    dve.wait_ge(s_add, k * 2 + 1)
                    nc.vector.tensor_tensor(acc_b, acc_b, sum_ps.rearrange("p (h c) -> p h c", h=H3),
                                            ALU.add).then_inc(s_add, 1)
                    dve.wait_ge(s_add, k * 2 + 2)

                def group(k, r, first, last):
                    ahead = not (last and r == U - 1)
                    at_pass(st, k, 1)
                    new_shift(k, r)
                    if not (first and r == 0):
                        add(k - 1, (r - 1) % U)
                    if ahead:
                        one_hot(k + 1, (r + 1) % U)
                    logits(k, r)
                    if ahead:
                        scores(k + 1, (r + 1) % U)
                    messages(k, r)
                    end_pass(st)
                one_hot(0, 0)
                scores(0, 0)
                groups_loop(dve, group)
                add(NG - 1, U - 1)


def attention_finish(nc, const, tag, x, h, acc, bv, wo, bo):
    with Phase(nc) as ctx:
        sb, pb, sem = memory(nc, ctx, tag)
        rec = sb("rec", [P, NB, H3])
        bvr = sb("bvr", [P, D])
        row = sb("row", [1, D])
        proj = Project(nc, ctx, const, tag + "proj", h, wo[:, :], row[:, :], D, 3)
        s_v, s_in, s_bv = sem("vector_step"), sem("loaded"), sem("bias_loaded")
        with nc.Block() as block:
            @block.sync
            def _(sp):
                sp.dma_start(row[:, :], bo.rearrange("(o d) -> o d", o=1)).then_inc(s_in, 16)
                sp.dma_start(bvr[:, :], bv.rearrange("(o d) -> o d", o=1).to_broadcast([P, D])).then_inc(s_bv, 16)

            @block.tensor
            def _(pe):
                pe.wait_ge(s_in, 16)
                proj.tensor(pe)

            @block.scalar
            def _(act):
                proj.scalar(act)

            @block.vector
            def _(dve):
                st = Steps(dve, s_v)
                dve.wait_ge(s_bv, 16)
                a = acc[:, :, :].rearrange("p b (h c) -> p b h c", h=H3)
                hv = h[:, :, :].rearrange("p b (h c) -> p b h c", h=H3)
                bvh = bvr[:, :].rearrange("p (h c) -> p h c", h=H3)
                for t in range(H3):
                    st.did(nc.vector.tensor_tensor(hv[:, :, t, :], a[:, :, t, HC3:HC3 + 1].to_broadcast([P, NB, HC3]),
                                                   bvh[:, t, :].unsqueeze(1).to_broadcast([P, NB, HC3]), ALU.mult))
                st.wait()
                for t in range(H3):
                    st.did(nc.vector.tensor_tensor(hv[:, :, t, :], hv[:, :, t, :], a[:, :, t, 0:HC3], ALU.add))
                st.did(nc.vector.tensor_scalar(rec[:, :, :], a[:, :, :, HC3], 1e-16, None, ALU.add))
                st.wait()
                st.did(nc.vector.reciprocal(rec[:, :, :], rec[:, :, :]))
                st.wait()
                hf = h[:, :, :].rearrange("p b (h c) -> p (b h) c", h=H3)
                st.did(nc.vector.tensor_tensor(hf, hf, rec[:, :, :].rearrange("p b h -> p (b h)").unsqueeze(2).to_broadcast([P, NB * H3, HC3]), ALU.mult))
                st.wait()
                dve.sem_inc(proj.s_h, 1)
                into_x(nc, proj, dve, x)


def program(nc, a, out):
    with Phase(nc) as ctx:
        const = constants(nc, ctx)
        sb, pb, sem = memory(nc, ctx)
        by_target = nc.dram_tensor("by_target", (SLOTS + PADS, 4), I32).ap()
        target_groups = sb("target_groups", [P, NG], I32)
        source_groups = sb("source_groups", [P, NG], I32)
        bucket_edges(nc, const, "t_", a["dst"], a["src"], by_target, target_groups)
        by_source = nc.dram_tensor("by_source", (SLOTS + PADS, 4), I32).ap()
        bucket_edges(nc, const, "s_", a["src"], a["dst"], by_source, source_groups)

        x = sb("x", [P, NB, D])
        h = sb("h", [P, NB, D])
        wx, bx = sb("wx", [P, WX]), sb("bx", [1, WX])
        tables = [nc.dram_tensor(f"table{n}", (NODES, TABW), F32).ap() for n in range(3)]
        h_rows = nc.dram_tensor("h_rows", (NODES, D), F32).ap()
        load_x(nc, a["x"], x)
        with Phase(nc) as gat:
            sb, pb, sem = memory(nc, gat, "gat_")
            ed, shift = sb("ed", [P, NB, H]), sb("shift", [P, NB, H])
            acc = sb("acc", [P, NB, ROW])
            gat_weights(nc, const, "w0f_", a["L0_gnn_W1"], a["L0_gnn_a_src1"], a["L0_gnn_a_dst1"], wx, bx)
            gat_nodes(nc, const, "n0f_", x, h, wx, bx, tables[0], ed, shift, acc, True)
            gat_edges(nc, const, "e0f_", by_target, target_groups, tables[0], ed, shift, acc)
            gat_finish(nc, "f0f_", x, acc, True, (a["L0_gnn_b1"],))
            gat_weights(nc, const, "w0b_", a["L0_gnn_W2"], a["L0_gnn_a_src2"], a["L0_gnn_a_dst2"], wx, bx)
            gat_nodes(nc, const, "n0b_", None, h, wx, bx, tables[1], ed, shift, acc, True)
            gat_edges(nc, const, "e0b_", by_source, source_groups, tables[1], ed, shift, acc)
            gat_finish(nc, "f0b_", x, acc, True, (a["L0_gnn_b2"],))
            w1, total = sb("w1", [P, D]), sb("total", [P, D])
            turned_weights(nc, const, "w1_", [(a["L1_gnn_W"], w1[:, :])])
            complement_nodes(nc, "n1_", x, h, h_rows, acc, const, total)
            sum_edges(nc, const, "e1_", by_target, target_groups, h_rows, acc)
            complement_finish(nc, const, "f1_", x, h, acc, total, w1, a["L1_gnn_b"])
            gat_weights(nc, const, "w2_", a["L2_gnn_lin_weight"], a["L2_gnn_att_src"], a["L2_gnn_att_dst"], wx, bx,
                        a["L2_gnn_coeffs_t"], a["L2_gnn_lin_bias"])
            gat_nodes(nc, const, "n2_", x, h, wx, bx, tables[2], ed, shift, acc, False)
            gat_edges(nc, const, "e2_", by_target, target_groups, tables[2], ed, shift, acc)
            gat_finish(nc, "f2_", x, acc, False)
        with Phase(nc) as att:
            sb, pb, sem = memory(nc, att, "att_")
            wk, wv, wo, qx, qb = sb("wk", [P, D]), sb("wv", [P, D]), sb("wo", [P, D]), sb("qx", [P, QW]), sb("qb", [1, QW])
            queries, shift, acc = sb("queries", [P, NB, QW]), sb("shift", [P, NB, H3]), sb("acc", [P, NB, ROW3])
            turned_weights(nc, const, "w3_", [(a["L3_gnn_Wk"], wk[:, :]), (a["L3_gnn_Wv"], wv[:, :]), (a["L3_gnn_Wo"], wo[:, :])])
            query_weights(nc, const, "wq_", a["L3_gnn_Wq"], a["L3_gnn_bq"], a["L3_gnn_bk"], qx, qb)
            attention_nodes(nc, const, "n3_", x, h, qx, qb, queries, shift, acc)
            attention_edges(nc, const, "e3_", by_source, source_groups, a["edge_attr_128"], a["edge_attr_128_n2"],
                            wk, wv, queries, shift, acc)
            attention_finish(nc, const, "f3_", x, h, acc, a["L3_gnn_bv"], wo, a["L3_gnn_bo"])
        store_x(nc, out, x)


_INS = ['x', 'src', 'dst', 'edge_attr_128', 'edge_attr_128_n2',
        'L0_gnn_W1', 'L0_gnn_a_src1', 'L0_gnn_a_dst1', 'L0_gnn_b1', 'L0_gnn_W2', 'L0_gnn_a_src2', 'L0_gnn_a_dst2',
        'L0_gnn_b2', 'L1_gnn_W', 'L1_gnn_b', 'L2_gnn_coeffs_t', 'L2_gnn_lin_weight', 'L2_gnn_lin_bias',
        'L2_gnn_att_src', 'L2_gnn_att_dst', 'L3_gnn_Wq', 'L3_gnn_bq', 'L3_gnn_Wk', 'L3_gnn_bk', 'L3_gnn_Wv',
        'L3_gnn_bv', 'L3_gnn_Wo', 'L3_gnn_bo']


def kernel(**inputs):
    import numpy as _np
    import concourse.bacc as _bacc
    from concourse import mybir as _mybir
    from concourse.bass_utils import run_bass_kernel_spmd as _run

    nc = _bacc.Bacc("TRN2", target_bir_lowering=False, num_devices=1)
    arrays, args = {}, {}
    for name in _INS:
        a = _np.ascontiguousarray(inputs[name])
        arrays[f"in_{name}"] = a
        args[name] = nc.dram_tensor(f"in_{name}", a.shape, _mybir.dt.from_np(a.dtype), kind="ExternalInput").ap()
    out = nc.dram_tensor("out", (N, D), _mybir.dt.float32, kind="ExternalOutput").ap()
    program(nc, args, out)
    return _run(nc, [arrays], core_ids=[0]).results[0]["out"]
```

```python
from contextlib import ExitStack

import concourse.bass as bass
from concourse import mybir

F32 = mybir.dt.float32
I32 = mybir.dt.int32
U32 = mybir.dt.uint32
BF16 = mybir.dt.bfloat16
ALU = mybir.AluOpType
ACT = mybir.ActivationFunctionType
AX = mybir.AxisListType

P = 128
N = 6250
E = 206250
D = 128
NB = -(-N // P)
NODES = NB * P
TAILN = N - (NB - 1) * P
G = 4
GE = G * P
NG = (E + NB * (GE - 1)) // GE
NG += -NG % 8
SLOTS = NG * GE
CH = 9
TC = -(-E // P)
TC += -TC % (2 * CH)
NCHUNK = TC // CH
TAIL = E - (P - 1) * TC
BK = NB + 1
PADS = P * TC - E
FAR = 1.0e30


class Steps:

    def __init__(self, engine, sem):
        self.engine, self.sem, self.now, self.n = engine, sem, 0, 0

    def did(self, instruction):
        instruction.then_inc(self.sem, 1)
        self.n += 1

    def wait(self):
        self.engine.wait_ge(self.sem, self.now + self.n)

    def enter(self, i, per, first=0):
        self.before, self.per = self.now + self.n, per
        self.now, self.n = i * per + (self.before - first * per), 0

    def leave(self, passes):
        assert self.n == self.per, (self.n, self.per)
        self.now, self.n = self.before + passes * self.per, 0


class Phase(ExitStack):

    def __init__(self, nc):
        super().__init__()
        self.nc, self.sems, self.borrowed = nc, [], []

    def borrow(self, sems):
        self.sems += sems
        self.borrowed += sems
        return sems

    def __exit__(self, *raised):
        if self.sems and raised[0] is None:
            with self.nc.Block() as block:
                @block.gpsimd
                def _(pool):
                    for s in self.borrowed:
                        pool.dma_reset(range(s.num, s.num + 1))
                    for s in self.sems:
                        pool.sem_clear(s)
        return super().__exit__(*raised)


def memory(nc, ctx, tag=""):
    def sb(name, shape, dt=F32):
        return ctx.enter_context(nc.sbuf_tensor(tag + name, shape, dt))

    def pb(name, shape, dt=F32):
        return ctx.enter_context(nc.psum_tensor(tag + name, shape, dt))

    def sem(name):
        ctx.sems.append(ctx.enter_context(nc.semaphore(tag + name)))
        return ctx.sems[-1]
    return sb, pb, sem


def constants(nc, ctx):
    sb, pb, sem = memory(nc, ctx)
    c = {
        "ident": sb("ident", [P, P]), "ones": sb("ones", [P, P]), "zeros": sb("zeros", [P, 512]),
        "ones_h": sb("ones_h", [P, P], BF16), "below_h": sb("below_h", [P, P], BF16),
        "zeros_h": sb("zeros_h", [P, 512], BF16), "lanes": sb("lanes", [P, P]), "lanes_i": sb("lanes_i", [P, P], I32),
        "groups": sb("groups_n", [P, NG]), "groups_i": sb("groups_ni", [P, NG], I32),
        "headmask": sb("headmask", [P, 4]), "headmask3": sb("headmask3", [P, 8]),
    }
    c["indirect"] = [sem(f"indirect{n}") for n in range(8)]
    s_set, s_made = sem("const_set"), sem("const_made")
    with nc.Block() as block:
        @block.vector
        def _(dve):
            nc.vector.memset(c["ones"][:, :], 1.0)
            nc.vector.memset(c["zeros"][:, :], 0.0)
            nc.vector.memset(c["ones_h"][:, :], 1.0)
            nc.vector.memset(c["zeros_h"][:, :], 0.0)
            nc.vector.memset(c["headmask"][:, :], 0.0).then_inc(s_set, 1)
            dve.wait_ge(s_set, 1)
            for h in range(4):
                nc.vector.memset(c["headmask"][32 * h:32 * h + 32, h:h + 1], 1.0)
            dve.wait_ge(s_made, 2)
            nc.vector.tensor_copy(c["lanes"][:, :], c["lanes_i"][:, :])
            nc.vector.tensor_copy(c["groups"][:, :], c["groups_i"][:, :])

        @block.gpsimd
        def _(pool):
            nc.gpsimd.iota(c["lanes_i"][:, :], [[1, P]], base=0, channel_multiplier=0).then_inc(s_made, 1)
            nc.gpsimd.iota(c["groups_i"][:, :], [[1, NG]], base=0, channel_multiplier=0).then_inc(s_made, 1)
            nc.gpsimd.memset(c["ident"][:, :], 0.0).then_inc(s_made, 1)
            nc.gpsimd.memset(c["below_h"][:, :], 1.0).then_inc(s_made, 1)
            nc.gpsimd.memset(c["headmask3"][:, :], 1.0).then_inc(s_made, 1)
            pool.wait_ge(s_made, 5)
            nc.gpsimd.affine_select(out=c["ident"][:, :], in_=c["ident"][:, :], compare_op=ALU.not_equal, fill=1.0,
                                    base=0, pattern=[[-1, P]], channel_multiplier=1).then_inc(s_made, 1)
            nc.gpsimd.affine_select(out=c["below_h"][:, :], in_=c["below_h"][:, :], compare_op=ALU.is_gt, fill=0.0,
                                    base=0, pattern=[[1, P]], channel_multiplier=-1).then_inc(s_made, 1)
            nc.gpsimd.affine_select(out=c["headmask3"][:, :], in_=c["headmask3"][:, :], compare_op=ALU.is_ge, fill=0.0,
                                    base=0, pattern=[[-16, 8]], channel_multiplier=1).then_inc(s_made, 1)
            pool.wait_ge(s_made, 8)
            nc.gpsimd.affine_select(out=c["headmask3"][:, :], in_=c["headmask3"][:, :], compare_op=ALU.is_ge, fill=0.0,
                                    base=15, pattern=[[16, 8]], channel_multiplier=-1).then_inc(s_made, 1)
            pool.wait_ge(s_made, 9)
    return c


def bucket_edges(nc, const, tag, key, other, slots, group_block):
    with Phase(nc) as ctx:
        sb, pb, sem = memory(nc, ctx, tag)
        key_i = sb("key_i", [P, TC], I32)
        other_i = sb("other_i", [P, TC], I32)
        key_block = sb("key_block", [P, TC])
        pay = sb("pay", [P, TC, 4], I32)
        empty = sb("empty", [P, SLOTS // P, 4], I32)
        hot = sb("hot", [P, 2, CH, BK], BF16)
        count = sb("count", [P, BK])
        whole = sb("whole", [P, BK], I32)
        last = sb("last", [P, BK])
        run = sb("run", [P, BK])
        gb_f = sb("gb_f", [P, 2, NG])
        ranked = sb("ranked", [P, CH, BK])
        pos_f = sb("pos_f", [P, CH])
        pos = sb("pos", [P, 2, CH], U32)
        send = sb("send", [P, 2, CH, 4], I32)
        hist = pb("hist", [P, 512])
        pre = pb("pre", [P, 2, 512])

        s_load, s_pad, s_numbered, s_empty = sem("loaded"), sem("padded"), sem("numbered"), sem("emptied")
        s_step, s_hot, s_hist, s_hist_end = sem("vector_step"), sem("hot_ready"), sem("hist_added"), sem("hist_done")
        s_hot2, s_pre, s_used = sem("hot2_ready"), sem("prefix_ready"), sem("prefix_used")
        s_pos, s_past, s_init = sem("slots_ready"), sem("pool_past_wait"), sem("slots_emptied")
        s_scat = ctx.borrow(const["indirect"][0:2])
        HALF = NCHUNK // 2

        with nc.Block() as block:
            @block.sync
            def _(sp):
                sp.wait_ge(s_pad, 1)
                for a, t in ((key, key_i), (other, other_i)):
                    sp.dma_start(t[0:P - 1, :], a[0:(P - 1) * TC].rearrange("(p c) -> p c", p=P - 1)).then_inc(s_load, 16)
                    sp.dma_start(t[P - 1:P, 0:TAIL], a[(P - 1) * TC:E].rearrange("(p c) -> p c", p=1)).then_inc(s_load, 16)
                sp.wait_ge(s_empty, 1)
                sp.dma_start(slots[0:SLOTS, :].rearrange("(p s) f -> p (s f)", p=P),
                             empty[:, :, :].rearrange("p s f -> p (s f)")).then_inc(s_init, 16)

            @block.gpsimd
            def _(pool):
                nc.gpsimd.iota(pay[:, :, 2], [[1, TC]], base=0, channel_multiplier=TC).then_inc(s_numbered, 1)
                nc.gpsimd.iota(pay[:, :, 3], [[0, TC]], base=0, channel_multiplier=0).then_inc(s_numbered, 1)
                pool.wait_ge(s_init, 16)
                with pool.Fori(0, HALF) as i:
                    for h in range(2):
                        pool.wait_ge(s_pos, i * 4 + (2 * h + 2))
                        pool.sem_inc(s_past, 1)
                        for c in range(CH):
                            nc.gpsimd.indirect_dma_start(
                                slots[:, :], bass.IndirectOffsetOnAxis(ap=pos[:, h, c:c + 1], axis=0),
                                send[:, h, c, :], None).then_inc(s_scat[h], 16)
                for h in range(2):
                    pool.wait_ge(s_scat[h], 16 * CH * HALF)

            @block.tensor
            def _(pe):
                flat = hist[:, 0:CH * BK]
                pe.matmul(flat, const["ones_h"][:, :], const["zeros_h"][:, 0:CH * BK], start=True, stop=False)
                with pe.Fori(0, HALF) as i:
                    for h in range(2):
                        pe.wait_ge(s_hot, i * 2 + (h + 1))
                        pe.matmul(flat, const["ones_h"][:, :], hot[:, h, :, :].rearrange("p c b -> p (c b)"),
                                  start=False, stop=False).then_inc(s_hist, 1)
                pe.matmul(flat, const["ones_h"][:, :], const["zeros_h"][:, 0:CH * BK], start=False,
                          stop=True).then_inc(s_hist_end, 1)
                with pe.Fori(0, HALF) as i:
                    for h in range(2):
                        pe.wait_ge(s_hot2, i * 2 + (h + 1))
                        pe.wait_ge(s_used, i * 2 + (h + 1))
                        pe.matmul(pre[:, h, 0:(CH + 1) * BK], const["ones_h"][:, :],
                                  const["zeros_h"][:, 0:(CH + 1) * BK], start=True, stop=False)
                        for c in range(CH):
                            pe.matmul(pre[:, h, (c + 1) * BK:(CH + 1) * BK].rearrange("p (c b) -> p c b", b=BK),
                                      const["ones_h"][:, :], hot[:, h, c:c + 1, :].to_broadcast([P, CH - c, BK]),
                                      start=False, stop=False)
                        pe.matmul(pre[:, h, 0:CH * BK], const["below_h"][:, :],
                                  hot[:, h, :, :].rearrange("p c b -> p (c b)"), start=False, stop=True).then_inc(s_pre, 1)

            @block.vector
            def _(dve):
                st = Steps(dve, s_step)
                st.did(nc.vector.memset(key_i[:, :], NODES))
                st.did(nc.vector.memset(other_i[:, :], 0))
                st.wait()
                nc.vector.memset(empty[:, :, 0].bitcast(F32), -1.0).then_inc(s_pad, 1)
                nc.vector.memset(empty[:, :, 1], NODES - 1)
                nc.vector.memset(empty[:, :, 2:4], 0).then_inc(s_empty, 1)
                dve.wait_ge(s_load, 64)
                st.did(nc.vector.tensor_copy(pay[:, :, 1], other_i[:, :]))
                st.wait()
                st.did(nc.vector.tensor_scalar(other_i[:, :], key_i[:, :], P - 1, None, ALU.bitwise_and))
                st.did(nc.vector.tensor_scalar(key_i[:, :], key_i[:, :], 7, None, ALU.arith_shift_right))
                st.wait()
                st.did(nc.vector.tensor_copy(pay[:, :, 0].bitcast(F32), other_i[:, :]))
                st.did(nc.vector.tensor_copy(key_block[:, :], key_i[:, :]))
                st.wait()

                def one_hot(i, h):
                    return nc.vector.tensor_tensor(
                        hot[:, h, :, :], key_block[:, bass.ds(i * (2 * CH) + h * CH, CH)].unsqueeze(2).to_broadcast([P, CH, BK]),
                        const["lanes"][:, 0:BK].unsqueeze(1).to_broadcast([P, CH, BK]), ALU.is_equal)

                dve.sem_inc(s_hist, 2)
                with dve.Fori(0, HALF) as i:
                    for h in range(2):
                        dve.wait_ge(s_hist, i * 2 + (h + 1))
                        one_hot(i, h).then_inc(s_hot, 1)
                dve.wait_ge(s_hist_end, 1)
                st.did(nc.vector.tensor_reduce(count[:, :], hist[:, 0:CH * BK].rearrange("p (c b) -> p b c", b=BK), AX.X, ALU.add))
                st.wait()
                st.did(nc.vector.tensor_scalar(whole[:, :], count[:, :], float(GE - 1), None, ALU.add))
                st.wait()
                st.did(nc.vector.tensor_scalar(whole[:, :], whole[:, :], GE.bit_length() - 1, None, ALU.arith_shift_right))
                st.wait()
                st.did(nc.vector.tensor_copy(count[:, :], whole[:, :]))
                st.wait()
                st.did(nc.vector.tensor_tensor_scan(last[:, :], const["ones"][:, 0:BK], count[:, :], 0.0, ALU.mult, ALU.add))
                st.wait()
                st.did(nc.vector.tensor_tensor(run[:, :], last[:, :], count[:, :], ALU.subtract))
                st.wait()
                st.did(nc.vector.tensor_scalar(run[:, :], run[:, :], float(GE), None, ALU.mult))
                st.wait()
                st.did(nc.vector.memset(run[:, NB:BK], float(SLOTS)))
                st.did(nc.vector.memset(gb_f[:, 1, :], 0.0))
                for b in range(NB - 1):
                    st.wait()
                    st.did(nc.vector.scalar_tensor_tensor(gb_f[:, b % 2, :], const["groups"][:, :], last[:, b:b + 1],
                                                          gb_f[:, (b + 1) % 2, :], ALU.is_ge, ALU.add))
                st.wait()
                st.did(nc.vector.tensor_copy(group_block[:, :], gb_f[:, (NB - 2) % 2, :]))
                st.wait()
                dve.wait_ge(s_numbered, 2)
                dve.sem_inc(s_used, 2)

                def rank_chunk(i, h, ring_used):
                    one_hot(i, h).then_inc(s_hot2, 1)
                    dve.wait_ge(s_pre, i * 2 + (h + 1))
                    st.did(nc.vector.tensor_tensor(
                        ranked[:, :, :], pre[:, h, 0:CH * BK].rearrange("p (c b) -> p c b", b=BK),
                        run[:, :].unsqueeze(1).to_broadcast([P, CH, BK]), ALU.add))
                    st.wait()
                    nc.vector.tensor_tensor(run[:, :], run[:, :], pre[:, h, CH * BK:(CH + 1) * BK],
                                            ALU.add).then_inc(s_used, 1)
                    st.did(nc.vector.tensor_tensor(ranked[:, :, :], ranked[:, :, :], hot[:, h, :, :], ALU.mult))
                    st.wait()
                    st.did(nc.vector.tensor_reduce(pos_f[:, :], ranked[:, :, :], AX.X, ALU.add))
                    st.wait()
                    if ring_used:
                        dve.wait_ge(s_scat[h], i * (16 * CH))
                    nc.vector.tensor_copy(pos[:, h, :], pos_f[:, :]).then_inc(s_pos, 1)
                    nc.vector.tensor_copy(send[:, h, :, :],
                                          pay[:, bass.ds(i * (2 * CH) + h * CH, CH), :]).then_inc(s_pos, 1)
                    dve.wait_ge(s_used, i * 2 + (h + 3))
                    dve.wait_ge(s_pos, i * 4 + (2 * h + 2))

                for h in range(2):
                    rank_chunk(0, h, False)
                with dve.Fori(1, HALF) as i:
                    st.enter(i, 6, 1)
                    for h in range(2):
                        rank_chunk(i, h, True)
                    st.leave(HALF - 1)


H = 4
HC = D // H
ROW = D + H
TABW = ROW + H
U = 4
RU = 8


def at_pass(steps, k, per):
    steps.now, steps.n, steps.per = k * per, 0, per


def end_pass(steps):
    assert steps.n == steps.per, (steps.n, steps.per)


def groups_loop(engine, body, unroll=U):
    for r in range(unroll):
        body(r, r, True, False)
    with engine.Fori(1, NG // unroll - 1) as i:
        for r in range(unroll):
            body(i * unroll + r, r, False, False)
    for r in range(unroll):
        body(NG - unroll + r, r, False, True)


def gat_edges(nc, const, tag, slots, group_block, table, ed, shift, acc):
    AHEAD = 3
    SHIFTS = 2
    with Phase(nc) as ctx:
        sb, pb, sem = memory(nc, ctx, tag)
        slot = sb("slot", [P, NG * G, 4], I32)
        idx = sb("idx", [P, RU, G], U32)
        rows = sb("rows", [P, RU, G, TABW])
        hot = sb("hot", [P, U, G, P])
        apart = sb("apart", [P, G * P])
        hot_t = sb("hot_t", [P, U, G * P])
        far = sb("far", [P, U, G * P])
        junk = sb("junk", [P, H, G * P], BF16)
        gmax = sb("gmax", [P, H])
        lin = sb("lin", [P, H])
        look = sb("look", [P, U, 2 * H])
        drop = sb("drop", [P, U, H])
        scale = sb("scale", [P, U, H])
        za = sb("za", [P, G, H])
        zb = sb("zb", [P, G, H])
        zc = sb("zc", [P, G, H])
        w = sb("w", [P, G, H])
        hot_ps = pb("hot_ps", [P, G * P])
        es_ps = pb("es_ps", [P, H, G * P])
        look_ps = pb("look_ps", [P, 2, 512])
        sum_ps = pb("sum_ps", [P, ROW])

        def looked_up(r):
            return look_ps[:, r % 2, 0:G * 2 * H].rearrange("p (j h) -> p j h", j=G)

        s_slot, s_idx, s_past = sem("slots_loaded"), sem("idx_ready"), sem("pool_past_wait")
        s_dpast, s_shift_step = sem("vector_past_wait"), sem("shift_step")
        s_rows = ctx.borrow(const["indirect"])
        s_apart, s_hot, s_hot_ps, s_hot_t, s_far = sem("distances"), sem("hot"), sem("hot_turned"), sem("hot_t_copied"), sem("far_ready")
        s_es, s_max, s_shift, s_look = sem("es_spread"), sem("max_taken"), sem("shift_ready"), sem("looked_up")
        s_drop, s_scale, s_z, s_w = sem("drop_ready"), sem("scale_ready"), sem("z_ready"), sem("w_ready")
        s_msg, s_sum, s_add, s_step = sem("messages"), sem("summed"), sem("added"), sem("vector_step")

        with nc.Block() as block:
            @block.sync
            def _(sp):
                sp.dma_start(slot[:, :, :].rearrange("p (g j) f -> p g (j f)", j=G),
                             slots[0:SLOTS, :].rearrange("(g p j) f -> p g (j f)", p=P, j=G)).then_inc(s_slot, 16)
                sp.wait_ge(s_slot, 16)

            @block.gpsimd
            def _(pool):
                def gather(k, r, first, last):
                    pool.wait_ge(s_idx, k + 1)
                    if not first:
                        pool.wait_ge(s_sum, k + (1 - RU))
                    pool.sem_inc(s_past, 1)
                    for j in range(G):
                        nc.gpsimd.indirect_dma_start(
                            rows[:, r, j, :], None, table[:, :],
                            bass.IndirectOffsetOnAxis(ap=idx[:, r, j:j + 1], axis=0)).then_inc(s_rows[r], 16)
                groups_loop(pool, gather, RU)
                for r in range(RU):
                    pool.wait_ge(s_rows[r], NG // RU * 16 * G)

            @block.scalar
            def _(act):
                act.wait_ge(s_slot, 16)

                def index(k, r, wait=True):
                    if wait:
                        act.wait_ge(s_rows[r], (k - r) * (16 * G // RU))
                    nc.scalar.copy(idx[:, r, :], slot[:, bass.ds(k * G, G), 1]).then_inc(s_idx, 1)

                def one_hot(k, r):
                    for j in range(G):
                        nc.scalar.activation(apart[:, j * P:(j + 1) * P], const["lanes"][:, :], ACT.Abs, scale=-1.0,
                                             bias=slot[:, bass.ds(k * G + j, 1), 0].bitcast(F32)).then_inc(s_apart, 1)
                    act.wait_ge(s_apart, k * G + G)
                    nc.scalar.activation(hot[:, r % U, :, :].rearrange("p j n -> p (j n)"), apart[:, :], ACT.Relu,
                                         bias=1.0, scale=-1.0).then_inc(s_hot, 1)

                def turned(k, r):
                    act.wait_ge(s_hot_ps, k + 1)
                    nc.scalar.copy(hot_t[:, r % U, :], hot_ps[:, :]).then_inc(s_hot_t, 1)
                    nc.scalar.activation(far[:, r % U, :], hot_ps[:, :], ACT.Copy, bias=-FAR,
                                         scale=FAR).then_inc(s_far, 1)

                def rescale(k, r):
                    act.wait_ge(s_drop, k + 1)
                    nc.scalar.activation(scale[:, r % U, :], drop[:, r % U, :], ACT.Exp).then_inc(s_scale, 1)

                def group(k, r, first, last):
                    if not last:
                        index(k + RU, r)
                    act.wait_ge(s_z, k + 1)
                    nc.scalar.activation(w[:, :, :], zc[:, :, :], ACT.Exp).then_inc(s_w, 1)
                    if not (last and r + AHEAD >= RU):
                        if not (first and r == 0):
                            act.wait_ge(s_sum, k)
                        one_hot(k + AHEAD, (r + AHEAD) % RU)
                        turned(k + AHEAD, (r + AHEAD) % RU)
                    if not (last and r + SHIFTS >= RU):
                        rescale(k + SHIFTS, (r + SHIFTS) % RU)
                for r in range(RU):
                    index(r, r, False)
                for r in range(AHEAD):
                    one_hot(r, r)
                    turned(r, r)
                for r in range(SHIFTS):
                    rescale(r, r)
                groups_loop(act, group, RU)

            @block.tensor
            def _(pe):
                def turn(k, r):
                    pe.wait_ge(s_hot, k + 1)
                    if not (isinstance(k, int) and k == 0):
                        pe.wait_ge(s_far, k)
                    for j in range(G):
                        mm = pe.transpose(hot_ps[:, j * P:(j + 1) * P], hot[:, r % U, j, :], const["ident"][:, :])
                    mm.then_inc(s_hot_ps, 1)

                def spread(k, r, free=True):
                    pe.wait_ge(s_rows[r], (k - r) * (16 * G // RU) + 16 * G)
                    for h in range(H):
                        if free:
                            pe.wait_ge(s_max, k * H + (h + 1 - H))
                        for j in range(G):
                            mm = pe.transpose(es_ps[:, h, j * P:(j + 1) * P],
                                              rows[:, r, j, ROW + h:ROW + h + 1].to_broadcast([P, P]), const["ident"][:, :])
                        mm.then_inc(s_es, 1)

                def look_up(k, r):
                    pe.wait_ge(s_shift, k * 2 + 2)
                    pe.wait_ge(s_hot_t, k + 1)
                    for j in range(G):
                        mm = pe.matmul(looked_up(r)[:, j, :], hot_t[:, r % U, j * P:(j + 1) * P], look[:, r % U, :],
                                       start=True, stop=True)
                    mm.then_inc(s_look, 1)

                def group(k, r, first, last):
                    pe.wait_ge(s_msg, k + 1)
                    for j in range(G):
                        mm = pe.matmul(sum_ps[:, :], hot[:, r % U, j, :], rows[:, r, j, 0:ROW],
                                       start=(j == 0), stop=(j == G - 1))
                    mm.then_inc(s_sum, 1)
                    if not (last and r + AHEAD >= RU):
                        turn(k + AHEAD, (r + AHEAD) % RU)
                        spread(k + AHEAD, (r + AHEAD) % RU)
                    if not (last and r + SHIFTS >= RU):
                        look_up(k + SHIFTS, (r + SHIFTS) % RU)
                for r in range(AHEAD):
                    turn(r, r)
                spread(0, 0, False)
                for r in range(SHIFTS):
                    spread(r + 1, r + 1)
                    look_up(r, r)
                groups_loop(pe, group, RU)

            @block.vector
            def _(dve):
                st, sh = Steps(dve, s_step), Steps(dve, s_shift_step)
                dve.wait_ge(s_slot, 16)

                def block_of(k):
                    return dve.value_load(group_block[0:1, bass.ds(k, 1)], min_val=0, max_val=NB - 1)

                def maximum(k, r, h):
                    if h == 0:
                        dve.wait_ge(s_far, k + 1)
                    dve.wait_ge(s_es, k * H + (h + 1))
                    dve.sem_inc(s_dpast, 1)
                    nc.vector.tensor_tensor_reduce(junk[:, h, :], es_ps[:, h, :], far[:, r % U, :], 1.0, -2 * FAR,
                                                   ALU.add, ALU.max, gmax[:, h:h + 1]).then_inc(s_max, 1)

                def new_shift(k, r, b):
                    at_pass(sh, k, 3)
                    ed_b = ed[:, bass.ds(b, 1), :].rearrange("p b h -> p (b h)")
                    shift_b = shift[:, bass.ds(b, 1), :].rearrange("p b h -> p (b h)")
                    nc.vector.tensor_copy(look[:, r % U, 0:H], ed_b).then_inc(s_shift, 1)
                    dve.wait_ge(s_max, k * H + H)
                    sh.did(nc.vector.tensor_tensor(gmax[:, :], gmax[:, :], ed_b, ALU.add))
                    sh.wait()
                    sh.did(nc.vector.scalar_tensor_tensor(lin[:, :], gmax[:, :], 0.2, gmax[:, :], ALU.mult, ALU.max))
                    sh.wait()
                    nc.vector.tensor_tensor(look[:, r % U, H:2 * H], lin[:, :], shift_b, ALU.max).then_inc(s_shift, 1)
                    dve.wait_ge(s_shift, k * 2 + 2)
                    nc.vector.tensor_tensor(drop[:, r % U, :], shift_b, look[:, r % U, H:2 * H],
                                            ALU.subtract).then_inc(s_drop, 1)
                    dve.wait_ge(s_drop, k + 1)
                    sh.did(nc.vector.tensor_scalar(shift_b, look[:, r % U, H:2 * H], 1.0, None, ALU.mult))
                    sh.wait()
                    end_pass(sh)

                def logits(k, r, add_in):
                    at_pass(st, k, 2)
                    dve.wait_ge(s_look, k + 1)
                    st.did(nc.vector.tensor_tensor(za[:, :, :], looked_up(r)[:, :, 0:H], rows[:, r, :, ROW:TABW], ALU.add))
                    add_in(0)
                    st.wait()
                    st.did(nc.vector.scalar_tensor_tensor(zb[:, :, :], za[:, :, :], 0.2, za[:, :, :], ALU.mult, ALU.max))
                    add_in(1)
                    st.wait()
                    nc.vector.tensor_tensor(zc[:, :, :], zb[:, :, :], looked_up(r)[:, :, H:2 * H],
                                            ALU.subtract).then_inc(s_z, 1)
                    end_pass(st)

                def messages(k, r):
                    dve.wait_ge(s_w, k + 1)
                    m = rows[:, r, :, 0:ROW].rearrange("p j (h c) -> p j h c", h=H)
                    nc.vector.tensor_tensor(m, m, w[:, :, :].unsqueeze(3).to_broadcast([P, G, H, HC + 1]),
                                            ALU.mult).then_inc(s_msg, 1)

                def add(k, r, b, step):
                    acc_b = acc[:, bass.ds(b, 1), :].rearrange("p b (h c) -> p (b h) c", h=H)
                    if step == 0:
                        dve.wait_ge(s_scale, k + 1)
                        nc.vector.tensor_tensor(acc_b, acc_b, scale[:, r % U, :].unsqueeze(2).to_broadcast([P, H, HC + 1]),
                                                ALU.mult).then_inc(s_add, 1)
                    else:
                        dve.wait_ge(s_sum, k + 1)
                        dve.wait_ge(s_add, k * 2 + 1)
                        nc.vector.tensor_tensor(acc_b, acc_b, sum_ps[:, :].rearrange("p (h c) -> p h c", h=H),
                                                ALU.add).then_inc(s_add, 1)

                blocks = {}

                def group(k, r, first, last):
                    if r == 0:
                        blocks.clear()
                    if first and r == 0:
                        logits(k, r, lambda step: None)
                    else:
                        b = blocks[r - 1] if r else block_of(k - 1)
                        logits(k, r, lambda step: add(k - 1, (r - 1) % RU, b, step))
                    ahead, r2 = not (last and r + SHIFTS >= RU), (r + SHIFTS) % RU
                    if ahead:
                        maximum(k + SHIFTS, r2, 0)
                    if not (first and r == 0):
                        dve.wait_ge(s_add, k * 2)
                    messages(k, r)
                    if ahead:
                        for h in range(1, H):
                            maximum(k + SHIFTS, r2, h)
                        blocks[r + SHIFTS] = block_of(k + SHIFTS)
                    if r not in blocks:
                        blocks[r] = block_of(k)
                    if ahead:
                        new_shift(k + SHIFTS, r2, blocks[r + SHIFTS])
                for r in range(SHIFTS):
                    for h in range(H):
                        maximum(r, r, h)
                    new_shift(r, r, block_of(r))
                groups_loop(dve, group, RU)
                for step in range(2):
                    add(NG - 1, RU - 1, block_of(NG - 1), step)
                dve.wait_ge(s_add, NG * 2)


def root(nc, act, m, s_var, s_std):
    act.wait_ge(s_var, 1)
    nc.scalar.activation(m[:, 1, :], m[:, 0, :], ACT.Sqrt).then_inc(s_std, 1)


def normed(nc, dve, st, x, h, sq, m, s_var, s_std):
    wide = [P, NB, D]
    st.did(nc.vector.tensor_reduce(m[:, 0, :], x[:, :, :], AX.X, ALU.add))
    st.wait()
    st.did(nc.vector.tensor_scalar(m[:, 0, :], m[:, 0, :], 1.0 / D, None, ALU.mult))
    st.wait()
    st.did(nc.vector.tensor_tensor(h[:, :, :], x[:, :, :], m[:, 0, :].unsqueeze(2).to_broadcast(wide), ALU.subtract))
    st.wait()
    st.did(nc.vector.tensor_tensor(sq, h[:, :, :], h[:, :, :], ALU.mult))
    st.wait()
    st.did(nc.vector.tensor_reduce(m[:, 1, :], sq, AX.X, ALU.add))
    st.wait()
    nc.vector.tensor_scalar(m[:, 0, :], m[:, 1, :], 1.0 / D, 1e-5, ALU.mult, ALU.add).then_inc(s_var, 1)
    dve.wait_ge(s_std, 1)
    st.did(nc.vector.reciprocal(m[:, 1, :], m[:, 1, :]))
    st.wait()
    st.did(nc.vector.scalar_tensor_tensor(h[:, :, :], h[:, :, :], 0.0, m[:, 1, :].unsqueeze(2).to_broadcast(wide),
                                          ALU.max, ALU.mult))
    st.wait()


class Project:
    B = 7

    def __init__(self, nc, ctx, const, tag, h, weight, bias, width, per):
        sb, pb, sem = memory(nc, ctx, tag)
        self.nc, self.const, self.h, self.weight, self.bias, self.width, self.per = nc, const, h, weight, bias, width, per
        self.ht_ps = pb("ht_ps", [P, 2, 512])
        self.stage = sb("stage", [P, self.B, D])
        self.ht = sb("ht", [P, self.B, P])
        self.out_ps = pb("out_ps", [P, 3, 512])
        self.s_h, self.s_turned, self.s_copied = sem("h_ready"), sem("h_turned"), sem("ht_copied")
        self.s_staged = sem("h_staged")
        self.s_ready, self.s_taken = sem("product_ready"), sem("product_taken")

    def product(self, n):
        return self.out_ps[:, n // 3, (n % 3) * self.width:(n % 3 + 1) * self.width]

    def products(self, bank):
        n = min(3, self.B - 3 * bank)
        return self.out_ps[:, bank, 0:n * self.width].rearrange("p (n w) -> p n w", w=self.width), 3 * bank, n

    def tensor(self, pe):
        with pe.Fori(0, NB // self.B) as i:
            pe.wait_ge(self.s_staged, i + 1)
            for n in range(self.B):
                mm = pe.transpose(self.ht_ps[:, n // 4, (n % 4) * P:(n % 4 + 1) * P],
                                  self.stage[:, n, :],
                                  self.const["ident"][:, :])
            mm.then_inc(self.s_turned, 1)
            pe.wait_ge(self.s_copied, i * 2 + 2)
            pe.wait_ge(self.s_taken, i * self.per + self.per)
            for n in range(self.B):
                if self.bias is not None:
                    pe.matmul(self.product(n), self.const["ones"][0:1, :], self.bias, start=True, stop=False)
                mm = pe.matmul(self.product(n), self.ht[:, n, :], self.weight, start=self.bias is None, stop=True)
            mm.then_inc(self.s_ready, 1)

    def scalar(self, act):
        act.wait_ge(self.s_h, 1)
        with act.Fori(0, NB // self.B) as i:
            self.nc.scalar.copy(self.stage[:, :, :], self.h[:, bass.ds(i * self.B, self.B), :]).then_inc(self.s_staged, 1)
            act.wait_ge(self.s_turned, i + 1)
            self.nc.scalar.copy(self.ht[:, 0:4, :].rearrange("p n d -> p (n d)"), self.ht_ps[:, 0, :]).then_inc(self.s_copied, 1)
            self.nc.scalar.copy(self.ht[:, 4:7, :].rearrange("p n d -> p (n d)"), self.ht_ps[:, 1, 0:3 * P]).then_inc(self.s_copied, 1)

    def vector(self, dve, take):
        dve.sem_inc(self.s_taken, self.per)
        with dve.Fori(0, NB // self.B) as i:
            dve.wait_ge(self.s_ready, i + 1)
            take(i)
        dve.wait_ge(self.s_taken, self.per * (NB // self.B + 1))


WX = TABW + H


def gat_weights(nc, const, tag, w_in, a_src, a_dst, wx, bx, coeffs=None, bias=None):
    n = 1 if coeffs is None else coeffs.shape[0]
    with Phase(nc) as ctx:
        sb, pb, sem = memory(nc, ctx, tag)
        raw = sb("raw", [P, n, D])
        att = sb("att", [P, 2, n])
        mix = sb("mix", [P, n])
        mixed = sb("mixed", [P, 2, D])
        vec = sb("vec", [P, 2, 2])
        braw = sb("braw", [P, n])
        bcol = sb("bcol", [P, 2])
        turned = sb("turned", [P, D])
        heads = sb("heads", [P, 2 * H])
        turn_ps = pb("turn_ps", [P, D])
        att_ps = pb("att_ps", [P, 2 * H])
        b_ps = pb("b_ps", [1, D])
        ba_ps = pb("ba_ps", [1, 2 * H])
        s_in, s_v, s_t, s_pe = sem("loaded"), sem("vector_step"), sem("heads_ready"), sem("turned")
        s_c = sem("turned_copied")
        loads = 3 if coeffs is None else 8
        with nc.Block() as block:
            @block.sync
            def _(sp):
                if coeffs is None:
                    sp.dma_start(raw[:, 0, :], w_in).then_inc(s_in, 16)
                    for v, t in ((a_src, 0), (a_dst, 1)):
                        sp.dma_start(att[:, t, :], v.rearrange("h (c o) -> (h c) o", o=1)).then_inc(s_in, 16)
                else:
                    sp.dma_start(raw[:, :, :], w_in.rearrange("n o i -> o n i")).then_inc(s_in, 16)
                    sp.dma_start(mix[:, :], coeffs.rearrange("(o n) -> o n", o=1).to_broadcast([P, n])).then_inc(s_in, 16)
                    for m in range(n):
                        for v, t in ((a_src, 0), (a_dst, 1)):
                            sp.dma_start(att[:, t, m:m + 1], v[m, 0].rearrange("h (c o) -> (h c) o", o=1)).then_inc(s_in, 16)
                        sp.dma_start(braw[:, m:m + 1], bias[m].rearrange("(d o) -> d o", o=1)).then_inc(s_in, 16)

            @block.tensor
            def _(pe):
                pe.wait_ge(s_t, 1)
                raw_w = raw[:, 0, :] if coeffs is None else mixed[:, (n - 1) % 2, :]
                pe.transpose(turn_ps[:, :], raw_w, const["ident"][:, :]).then_inc(s_pe, 1)
                pe.wait_ge(s_c, 1)
                by_out = turned[:, :] if coeffs is None else raw_w
                pe.matmul(att_ps[:, :], by_out, heads[:, :], start=True, stop=True).then_inc(s_pe, 1)
                if coeffs is not None:
                    pe.matmul(b_ps[:, :], bcol[:, (n - 1) % 2:(n - 1) % 2 + 1], const["ident"][:, :], start=True, stop=True)
                    pe.matmul(ba_ps[:, :], bcol[:, (n - 1) % 2:(n - 1) % 2 + 1], heads[:, :], start=True, stop=True).then_inc(s_pe, 1)

            @block.vector
            def _(dve):
                st = Steps(dve, s_v)
                dve.wait_ge(s_in, 16 * (3 if coeffs is None else 2 + 3 * n))
                if coeffs is None:
                    srcs = [att[:, 0, 0:1], att[:, 1, 0:1]]
                else:
                    for m in range(n):
                        at, fr = m % 2, (m + 1) % 2
                        for dst, new, old in [(mixed[:, at, :], raw[:, m, :], mixed[:, fr, :]),
                                              (bcol[:, at:at + 1], braw[:, m:m + 1], bcol[:, fr:fr + 1]),
                                              (vec[:, 0, at:at + 1], att[:, 0, m:m + 1], vec[:, 0, fr:fr + 1]),
                                              (vec[:, 1, at:at + 1], att[:, 1, m:m + 1], vec[:, 1, fr:fr + 1])]:
                            if m == 0:
                                st.did(nc.vector.tensor_scalar(dst, new, mix[:, 0:1], None, ALU.mult))
                            else:
                                st.did(nc.vector.scalar_tensor_tensor(dst, new, mix[:, m:m + 1], old, ALU.mult, ALU.add))
                        st.wait()
                    at = (n - 1) % 2
                    srcs = [vec[:, 0, at:at + 1], vec[:, 1, at:at + 1]]
                for t in range(2):
                    st.did(nc.vector.tensor_scalar(heads[:, t * H:(t + 1) * H], const["headmask"][:, :], srcs[t], None, ALU.mult))
                st.did(nc.vector.memset(wx[:, :], 0.0))
                st.did(nc.vector.memset(bx[:, :], 0.0))
                st.wait()
                st.did(nc.vector.memset(bx[:, HC:ROW:HC + 1], 1.0))
                st.wait()
                dve.sem_inc(s_t, 1)
                dve.wait_ge(s_pe, 1)
                nc.vector.tensor_copy(turned[:, :], turn_ps[:, :]).then_inc(s_c, 1)
                cols = wx[:, 0:ROW].rearrange("p (h c) -> p h c", h=H)[:, :, 0:HC]
                by_in = raw[:, 0, :] if coeffs is None else turn_ps[:, :]
                st.did(nc.vector.tensor_copy(cols, by_in.rearrange("p (h c) -> p h c", h=H)))
                dve.wait_ge(s_pe, 2)
                st.did(nc.vector.tensor_copy(wx[:, ROW:WX], att_ps[:, :]))
                if coeffs is not None:
                    dve.wait_ge(s_pe, 3)
                    st.did(nc.vector.tensor_copy(bx[:, 0:ROW].rearrange("p (h c) -> p h c", h=H)[:, :, 0:HC],
                                                 b_ps[:, :].rearrange("p (h c) -> p h c", h=H)))
                    st.did(nc.vector.tensor_copy(bx[:, ROW:WX], ba_ps[:, :]))
                st.wait()


def gat_nodes(nc, const, tag, x, h, wx, bx, table, ed, shift, acc, loops):
    with Phase(nc) as ctx:
        sb, pb, sem = memory(nc, ctx, tag)
        rows = sb("rows", [P, NB, TABW])
        m = sb("moments", [P, 2, NB])
        lin = sb("lin", [P, NB, H])
        proj = Project(nc, ctx, const, tag + "proj", h, wx[:, :], bx[:, :], WX, 6)
        s_v, s_out = sem("vector_step"), sem("table_out")
        s_rows, s_var, s_std = sem("rows_ready"), sem("variance"), sem("deviation")
        with nc.Block() as block:
            @block.sync
            def _(sp):
                sp.wait_ge(s_rows, 1)
                sp.dma_start(table.rearrange("(b p) f -> p b f", p=P), rows[:, :, :]).then_inc(s_out, 16)
                sp.wait_ge(s_out, 16)

            @block.tensor
            def _(pe):
                proj.tensor(pe)

            @block.scalar
            def _(act):
                if x is not None:
                    root(nc, act, m, s_var, s_std)
                proj.scalar(act)

            @block.vector
            def _(dve):
                st = Steps(dve, s_v)
                if x is not None:
                    normed(nc, dve, st, x, h, acc[:, :, 0:D], m, s_var, s_std)
                dve.sem_inc(proj.s_h, 1)

                def take(i):
                    for bank in range(3):
                        ps, n0, n = proj.products(bank)
                        b = bass.ds(i * proj.B + n0, n)
                        nc.vector.tensor_scalar(rows[:, b, :], ps[:, :, 0:TABW], 1.0, None, ALU.mult).then_inc(proj.s_taken, 1)
                        nc.vector.tensor_copy(ed[:, b, :], ps[:, :, TABW:WX]).then_inc(proj.s_taken, 1)
                proj.vector(dve, take)
                dve.sem_inc(s_rows, 1)
                if loops:
                    st.did(nc.vector.tensor_copy(acc[:, :, :], rows[:, :, 0:ROW]))
                    st.did(nc.vector.tensor_tensor(lin[:, :, :], rows[:, :, ROW:TABW], ed[:, :, :], ALU.add))
                    st.wait()
                    st.did(nc.vector.scalar_tensor_tensor(shift[:, :, :], lin[:, :, :], 0.2, lin[:, :, :], ALU.mult, ALU.max))
                else:
                    st.did(nc.vector.memset(acc[:, :, :], 0.0))
                    st.did(nc.vector.memset(shift[:, :, :], -FAR))
                st.wait()


def gat_finish(nc, tag, x, acc, half, rows=()):
    with Phase(nc) as ctx:
        sb, pb, sem = memory(nc, ctx, tag)
        rec = sb("rec", [P, NB * H])
        add = sb("add", [P, D])
        s_in, s_v = sem("loaded"), sem("vector_step")
        with nc.Block() as block:
            @block.sync
            def _(sp):
                for row in rows:
                    sp.dma_start(add[:, :], row.rearrange("(o d) -> o d", o=1).to_broadcast([P, D])).then_inc(s_in, 16)

            @block.vector
            def _(dve):
                st = Steps(dve, s_v)
                a = acc[:, :, :].rearrange("p b (h c) -> p (b h) c", h=H)
                if half:
                    st.did(nc.vector.reciprocal(rec[:, :], a[:, :, HC]))
                    st.wait()
                    st.did(nc.vector.tensor_scalar(rec[:, :], rec[:, :], 0.5, None, ALU.mult))
                else:
                    st.did(nc.vector.tensor_scalar(rec[:, :], a[:, :, HC], 1e-16, None, ALU.add))
                    st.wait()
                    st.did(nc.vector.reciprocal(rec[:, :], rec[:, :]))
                st.wait()
                st.did(nc.vector.tensor_tensor(a[:, :, 0:HC], a[:, :, 0:HC],
                                               rec[:, :].unsqueeze(2).to_broadcast([P, NB * H, HC]), ALU.mult))
                st.wait()
                xv = x[:, :, :].rearrange("p b (h c) -> p (b h) c", h=H)
                st.did(nc.vector.tensor_tensor(xv, xv, a[:, :, 0:HC], ALU.add))
                st.wait()
                if rows:
                    dve.wait_ge(s_in, 16)
                    st.did(nc.vector.tensor_scalar(add[:, :], add[:, :], 0.5, None, ALU.mult))
                    st.wait()
                    st.did(nc.vector.tensor_tensor(x[:, :, :], x[:, :, :], add[:, :].unsqueeze(1).to_broadcast([P, NB, D]),
                                                   ALU.add))
                    st.wait()


def load_x(nc, a, x):
    with Phase(nc) as ctx:
        sb, pb, sem = memory(nc, ctx, "x_")
        s_in, s_pad = sem("loaded"), sem("padded")
        with nc.Block() as block:
            @block.vector
            def _(dve):
                nc.vector.memset(x[:, NB - 1, :], 0.0).then_inc(s_pad, 1)

            @block.sync
            def _(sp):
                sp.dma_start(x[:, 0:NB - 1, :], a[0:(NB - 1) * P, :].rearrange("(b p) d -> p b d", p=P)).then_inc(s_in, 16)
                sp.wait_ge(s_pad, 1)
                sp.dma_start(x[0:TAILN, NB - 1, :], a[(NB - 1) * P:N, :]).then_inc(s_in, 16)
                sp.wait_ge(s_in, 32)


def store_x(nc, out, x):
    with Phase(nc) as ctx:
        sb, pb, sem = memory(nc, ctx, "out_")
        s_out = sem("stored")
        with nc.Block() as block:
            @block.sync
            def _(sp):
                sp.dma_start(out[0:(NB - 1) * P, :].rearrange("(b p) d -> p b d", p=P), x[:, 0:NB - 1, :]).then_inc(s_out, 16)
                sp.dma_start(out[(NB - 1) * P:N, :], x[0:TAILN, NB - 1, :]).then_inc(s_out, 16)
                sp.wait_ge(s_out, 32)


def sum_edges(nc, const, tag, slots, group_block, table, acc):
    with Phase(nc) as ctx:
        sb, pb, sem = memory(nc, ctx, tag)
        slot = sb("slot", [P, NG * G, 4], I32)
        idx = sb("idx", [P, U, G], U32)
        rows = sb("rows", [P, U, G, D])
        hot = sb("hot", [P, U, G, P])
        sum_ps = pb("sum_ps", [P, U, 512])
        s_slot, s_idx, s_past = sem("slots_loaded"), sem("idx_ready"), sem("pool_past_wait")
        s_rows = ctx.borrow(const["indirect"][0:U])
        s_hot, s_sum, s_add = sem("hot"), sem("summed"), sem("added")

        with nc.Block() as block:
            @block.sync
            def _(sp):
                sp.dma_start(slot[:, :, :].rearrange("p (g j) f -> p g (j f)", j=G),
                             slots[0:SLOTS, :].rearrange("(g p j) f -> p g (j f)", p=P, j=G)).then_inc(s_slot, 16)
                sp.wait_ge(s_slot, 16)

            @block.gpsimd
            def _(pool):
                def gather(k, r, first, last):
                    pool.wait_ge(s_idx, k + 1)
                    if not first:
                        pool.wait_ge(s_sum, k + (1 - U))
                    pool.sem_inc(s_past, 1)
                    for j in range(G):
                        nc.gpsimd.indirect_dma_start(
                            rows[:, r, j, :], None, table[:, :],
                            bass.IndirectOffsetOnAxis(ap=idx[:, r, j:j + 1], axis=0)).then_inc(s_rows[r], 16)
                groups_loop(pool, gather)
                for r in range(U):
                    pool.wait_ge(s_rows[r], NG // U * 16 * G)

            @block.scalar
            def _(act):
                act.wait_ge(s_slot, 16)

                def index(k, r, first, last):
                    if not first:
                        act.wait_ge(s_rows[r], (k - r) * (16 * G // U))
                    nc.scalar.copy(idx[:, r, :], slot[:, bass.ds(k * G, G), 1]).then_inc(s_idx, 1)
                groups_loop(act, index)

            @block.tensor
            def _(pe):
                def add_up(k, r, first, last):
                    pe.wait_ge(s_rows[r], (k - r) * (16 * G // U) + 16 * G)
                    pe.wait_ge(s_hot, k + 1)
                    if not first:
                        pe.wait_ge(s_add, k + (1 - U))
                    for j in range(G):
                        mm = pe.matmul(sum_ps[:, r, 0:D], hot[:, r, j, :], rows[:, r, j, :],
                                       start=(j == 0), stop=(j == G - 1))
                    mm.then_inc(s_sum, 1)
                groups_loop(pe, add_up)

            @block.vector
            def _(dve):
                dve.wait_ge(s_slot, 16)

                def one_hot(k, r):
                    nc.vector.tensor_tensor(
                        hot[:, r, :, :], const["lanes"][:, :].unsqueeze(1).to_broadcast([P, G, P]),
                        slot[:, bass.ds(k * G, G), 0].bitcast(F32).unsqueeze(2).to_broadcast([P, G, P]),
                        ALU.is_equal).then_inc(s_hot, 1)

                def group(k, r, first, last):
                    b = dve.value_load(group_block[0:1, bass.ds(k, 1)], min_val=0, max_val=NB - 1)
                    if not (last and r >= 2):
                        if not (first and r < 2):
                            dve.wait_ge(s_sum, k + (3 - U))
                        one_hot(k + 2, (r + 2) % U)
                    acc_b = acc[:, bass.ds(b, 1), 0:D].rearrange("p b d -> p (b d)")
                    if not (first and r == 0):
                        dve.wait_ge(s_add, k)
                    dve.wait_ge(s_sum, k + 1)
                    nc.vector.tensor_tensor(acc_b, acc_b, sum_ps[:, r, 0:D], ALU.add).then_inc(s_add, 1)
                for r in range(2):
                    one_hot(r, r)
                groups_loop(dve, group)


def turned_weights(nc, const, tag, pairs):
    with Phase(nc) as ctx:
        sb, pb, sem = memory(nc, ctx, tag)
        raw = sb("raw", [P, len(pairs), D])
        ps = pb("ps", [P, 4, P])
        assert len(pairs) <= 4
        s_in, s_pe = sem("loaded"), sem("turned")
        with nc.Block() as block:
            @block.sync
            def _(sp):
                for n, (w, t) in enumerate(pairs):
                    sp.dma_start(raw[:, n, :], w).then_inc(s_in, 16)

            @block.tensor
            def _(pe):
                pe.wait_ge(s_in, 16 * len(pairs))
                for n in range(len(pairs)):
                    pe.transpose(ps[:, n, :], raw[:, n, :], const["ident"][:, :]).then_inc(s_pe, 1)

            @block.vector
            def _(dve):
                dve.wait_ge(s_pe, len(pairs))
                for n, (w, t) in enumerate(pairs):
                    nc.vector.tensor_copy(t, ps[:, n, :])


def complement_nodes(nc, tag, x, h, table, acc, const, total):
    with Phase(nc) as ctx:
        sb, pb, sem = memory(nc, ctx, tag)
        m = sb("moments", [P, 2, NB])
        ps = pb("ps", [P, D])
        s_v, s_out, s_h, s_pe = sem("vector_step"), sem("table_out"), sem("h_ready"), sem("total_ready")
        s_var, s_std = sem("variance"), sem("deviation")
        with nc.Block() as block:
            @block.sync
            def _(sp):
                sp.wait_ge(s_h, 1)
                sp.dma_start(table.rearrange("(b p) f -> p b f", p=P), h[:, :, :]).then_inc(s_out, 16)
                sp.wait_ge(s_out, 16)

            @block.scalar
            def _(act):
                root(nc, act, m, s_var, s_std)

            @block.tensor
            def _(pe):
                pe.wait_ge(s_h, 1)
                pe.matmul(ps[:, :], const["ones"][:, :], h[:, 0, :], start=True, stop=False)
                with pe.Fori(0, (NB - 3) // 2) as i:
                    for n in range(2):
                        pe.matmul(ps[:, :], const["ones"][:, :], h[:, bass.ds(i * 2 + (n + 1), 1), :].rearrange("p b d -> p (b d)"),
                                  start=False, stop=False)
                pe.matmul(ps[:, :], const["ones"][:, :], h[:, NB - 2, :], start=False, stop=False)
                pe.matmul(ps[:, :], const["ones"][0:TAILN, :], h[0:TAILN, NB - 1, :], start=False, stop=True).then_inc(s_pe, 1)

            @block.vector
            def _(dve):
                st = Steps(dve, s_v)
                normed(nc, dve, st, x, h, acc[:, :, 0:D], m, s_var, s_std)
                dve.sem_inc(s_h, 1)
                st.did(nc.vector.memset(acc[:, :, :], 0.0))
                dve.wait_ge(s_pe, 1)
                st.did(nc.vector.tensor_copy(total[:, :], ps[:, :]))
                st.wait()


def into_x(nc, proj, dve, x):
    def take(i):
        for bank in range(3):
            ps, n0, n = proj.products(bank)
            xb = x[:, bass.ds(i * proj.B + n0, n), :]
            nc.vector.tensor_tensor(xb, xb, ps, ALU.add).then_inc(proj.s_taken, 1)
    proj.vector(dve, take)


def complement_finish(nc, const, tag, x, h, acc, total, weight, bias):
    with Phase(nc) as ctx:
        sb, pb, sem = memory(nc, ctx, tag)
        n2 = sb("norm", [P, 2, NB])
        row = sb("row", [1, D])
        proj = Project(nc, ctx, const, tag + "proj", h, weight[:, :], row[:, :], D, 3)
        s_v, s_in, s_sq, s_root = sem("vector_step"), sem("loaded"), sem("squares"), sem("roots")
        with nc.Block() as block:
            @block.sync
            def _(sp):
                sp.dma_start(row[:, :], bias.rearrange("(o d) -> o d", o=1)).then_inc(s_in, 16)

            @block.tensor
            def _(pe):
                pe.wait_ge(s_in, 16)
                proj.tensor(pe)

            @block.scalar
            def _(act):
                act.wait_ge(s_sq, 1)
                nc.scalar.activation(n2[:, 1, :], n2[:, 0, :], ACT.Sqrt).then_inc(s_root, 1)
                proj.scalar(act)

            @block.vector
            def _(dve):
                st = Steps(dve, s_v)
                wide = [P, NB, D]
                sq = acc[:, :, 0:D]
                st.did(nc.vector.tensor_tensor(h[:, :, :], total[:, :].unsqueeze(1).to_broadcast(wide), acc[:, :, 0:D], ALU.subtract))
                st.wait()
                st.did(nc.vector.tensor_tensor(sq, h[:, :, :], h[:, :, :], ALU.mult))
                st.wait()
                nc.vector.tensor_reduce(n2[:, 0, :], sq, AX.X, ALU.add).then_inc(s_sq, 1)
                dve.wait_ge(s_root, 1)
                st.did(nc.vector.tensor_scalar(n2[:, 1, :], n2[:, 1, :], 1e-12, None, ALU.max))
                st.wait()
                st.did(nc.vector.reciprocal(n2[:, 1, :], n2[:, 1, :]))
                st.wait()
                st.did(nc.vector.tensor_tensor(h[:, :, :], h[:, :, :], n2[:, 1, :].unsqueeze(2).to_broadcast(wide), ALU.mult))
                st.wait()
                dve.sem_inc(proj.s_h, 1)
                into_x(nc, proj, dve, x)


H3 = 8
HC3 = D // H3
ROW3 = D + H3
QW = D + H3


def query_weights(nc, const, tag, wq, bq, bk, qx, qb):
    with Phase(nc) as ctx:
        sb, pb, sem = memory(nc, ctx, tag)
        raw = sb("raw", [P, D])
        cols = sb("cols", [P, 2])
        heads = sb("heads", [P, H3])
        ps = pb("ps", [P, D])
        ps_h = pb("ps_h", [P, H3])
        ps_b = pb("ps_b", [1, D + H3])
        s_in, s_v, s_t, s_pe = sem("loaded"), sem("vector_step"), sem("scaled"), sem("products")
        with nc.Block() as block:
            @block.sync
            def _(sp):
                sp.dma_start(raw[:, :], wq).then_inc(s_in, 16)
                sp.dma_start(cols[:, 0:1], bq.rearrange("(d o) -> d o", o=1)).then_inc(s_in, 16)
                sp.dma_start(cols[:, 1:2], bk.rearrange("(d o) -> d o", o=1)).then_inc(s_in, 16)

            @block.tensor
            def _(pe):
                pe.wait_ge(s_t, 3)
                pe.transpose(ps[:, :], raw[:, :], const["ident"][:, :])
                pe.matmul(ps_h[:, :], raw[:, :], heads[:, :], start=True, stop=True)
                pe.matmul(ps_b[:, 0:D], cols[:, 0:1], const["ident"][:, :], start=True, stop=True)
                pe.matmul(ps_b[:, D:QW], cols[:, 0:1], heads[:, :], start=True, stop=True).then_inc(s_pe, 1)

            @block.vector
            def _(dve):
                dve.wait_ge(s_in, 48)
                scale = float(HC3) ** -0.5
                nc.vector.tensor_scalar(heads[:, :], const["headmask3"][:, :], cols[:, 1:2], None, ALU.mult).then_inc(s_t, 1)
                nc.vector.tensor_scalar(raw[:, :], raw[:, :], scale, None, ALU.mult).then_inc(s_t, 1)
                nc.vector.tensor_scalar(cols[:, 0:1], cols[:, 0:1], scale, None, ALU.mult).then_inc(s_t, 1)
                dve.wait_ge(s_pe, 1)
                nc.vector.tensor_copy(qx[:, 0:D], ps[:, :]).then_inc(s_v, 1)
                nc.vector.tensor_copy(qx[:, D:QW], ps_h[:, :]).then_inc(s_v, 1)
                nc.vector.tensor_copy(qb[:, :], ps_b[:, :]).then_inc(s_v, 1)
                dve.wait_ge(s_v, 3)


def attention_nodes(nc, const, tag, x, h, qx, qb, queries, shift, acc):
    with Phase(nc) as ctx:
        sb, pb, sem = memory(nc, ctx, tag)
        m = sb("moments", [P, 2, NB])
        proj = Project(nc, ctx, const, tag + "proj", h, qx[:, :], qb[:, :], QW, 3)
        s_v, s_var, s_std = sem("vector_step"), sem("variance"), sem("deviation")
        with nc.Block() as block:
            @block.tensor
            def _(pe):
                proj.tensor(pe)

            @block.scalar
            def _(act):
                root(nc, act, m, s_var, s_std)
                proj.scalar(act)

            @block.vector
            def _(dve):
                st = Steps(dve, s_v)
                normed(nc, dve, st, x, h, acc[:, :, 0:D], m, s_var, s_std)
                dve.sem_inc(proj.s_h, 1)

                def take(i):
                    for bank in range(3):
                        ps, n0, n = proj.products(bank)
                        nc.vector.tensor_scalar(queries[:, bass.ds(i * proj.B + n0, n), :], ps, 1.0, None,
                                                ALU.mult).then_inc(proj.s_taken, 1)
                proj.vector(dve, take)
                st.did(nc.vector.memset(acc[:, :, :], 0.0))
                st.did(nc.vector.memset(shift[:, :, :], -FAR))
                st.wait()


def attention_edges(nc, const, tag, slots, group_block, keys, values, wk, wv, queries, shift, acc):
    with Phase(nc) as ctx:
        sb, pb, sem = memory(nc, ctx, tag)
        slot = sb("slot", [P, NG * G, 4], I32)
        idx = sb("idx", [P, U, G], U32)
        krow = sb("krow", [P, 2, G, D])
        vrow = sb("vrow", [P, 2, G, D])
        hot = sb("hot", [P, U, G, P])
        hot_t = sb("hot_t", [P, 2, G * P])
        far = sb("far", [P, 2, G * P])
        krow_t = sb("krow_t", [P, G * P])
        vrow_t = sb("vrow_t", [P, G * P])
        key = sb("key", [P, G * D])
        value = sb("value", [P, 2, G * H3, HC3 + 1])
        prod = sb("prod", [P, G * D])
        score = sb("score", [P, 2, G, H3])
        junk = sb("junk", [P, 2, G * P], BF16)
        query = sb("query", [P, 2, D])
        gmax = sb("gmax", [P, H3])
        top = sb("top", [P, H3])
        new = sb("new", [P, 2, H3])
        drop = sb("drop", [P, 2, H3])
        scale = sb("scale", [P, 2, H3])
        z = sb("z", [P, G, H3])
        w = sb("w", [P, G * H3])
        msg = sb("msg", [P, G * H3, HC3 + 1])
        hot_ps = pb("hot_ps", [P, G * P])
        row_ps = pb("row_ps", [P, G * P])
        key_ps = pb("key_ps", [P, G * D])
        value_ps = pb("value_ps", [P, G * D])
        query_ps = pb("query_ps", [P, G * D])
        spread_ps = pb("spread_ps", [P, 2, G * P])
        misc_ps = pb("misc_ps", [P, 512])
        new_ps = misc_ps[:, 0:G * H3].rearrange("p (j h) -> p j h", j=G)
        sum_ps = misc_ps[:, 128:128 + ROW3]

        s_slot, s_idx, s_past = sem("slots_loaded"), sem("idx_ready"), sem("pool_past_wait")
        s_krow, s_vrow = ctx.borrow(const["indirect"][0:2]), ctx.borrow(const["indirect"][2:4])
        s_hot, s_hot_ps, s_hot_t, s_far = sem("hot"), sem("hot_turned"), sem("hot_t_copied"), sem("far_ready")
        s_row_ps, s_row_t, s_key_ps, s_key = sem("row_turned"), sem("row_t_copied"), sem("key_product"), sem("key_copied")
        s_value_ps, s_value, s_ones = sem("value_product"), sem("value_copied"), sem("ones_set")
        s_query, s_query_ps, s_prod, s_score = sem("query_copied"), sem("queries_looked_up"), sem("product_taken"), sem("score_ready")
        s_spread, s_max, s_new, s_new_ps = sem("score_spread"), sem("max_taken"), sem("shift_ready"), sem("shift_looked_up")
        s_drop, s_scale, s_z, s_w = sem("drop_ready"), sem("scale_ready"), sem("z_ready"), sem("w_ready")
        s_msg, s_sum, s_add, s_step, s_dpast = sem("messages"), sem("summed"), sem("added"), sem("vector_step"), sem("vector_past_wait")

        with nc.Block() as block:
            @block.sync
            def _(sp):
                sp.dma_start(slot[:, :, :].rearrange("p (g j) f -> p g (j f)", j=G),
                             slots[0:SLOTS, :].rearrange("(g p j) f -> p g (j f)", p=P, j=G)).then_inc(s_slot, 16)
                sp.wait_ge(s_slot, 16)

            @block.gpsimd
            def _(pool):
                def gather(k, r, first, last):
                    pool.wait_ge(s_idx, k + 1)
                    if not (first and r < 2):
                        pool.wait_ge(s_row_ps, k * 2 - 2)
                    pool.sem_inc(s_past, 1)
                    for t, ring, s in ((keys, krow, s_krow), (values, vrow, s_vrow)):
                        for j in range(G):
                            nc.gpsimd.indirect_dma_start(
                                ring[:, r % 2, j, :], None, t[:, :],
                                bass.IndirectOffsetOnAxis(ap=idx[:, r, j:j + 1], axis=0)).then_inc(s[r % 2], 16)
                groups_loop(pool, gather)
                for r in range(2):
                    pool.wait_ge(s_krow[r], NG // 2 * 16 * G)
                    pool.wait_ge(s_vrow[r], NG // 2 * 16 * G)

            @block.scalar
            def _(act):
                act.wait_ge(s_slot, 16)

                def index(k, r, wait=True):
                    if wait:
                        act.wait_ge(s_vrow[r % 2], (k - r) * (16 * G // 2) + (r // 2 - U // 2 + 1) * 16 * G)
                    nc.scalar.copy(idx[:, r, :], slot[:, bass.ds(k * G, G), 2]).then_inc(s_idx, 1)

                def key_rows(k, r):
                    act.wait_ge(s_row_ps, k * 2 + 1)
                    nc.scalar.copy(krow_t[:, :], row_ps[:, :]).then_inc(s_row_t, 1)

                def turned(k, r):
                    act.wait_ge(s_hot_ps, k + 1)
                    nc.scalar.copy(hot_t[:, r % 2, :], hot_ps[:, :]).then_inc(s_hot_t, 1)
                    nc.scalar.activation(far[:, r % 2, :], hot_ps[:, :], ACT.Copy, bias=-FAR, scale=FAR).then_inc(s_far, 1)

                def value_rows(k, r):
                    act.wait_ge(s_row_ps, k * 2 + 2)
                    nc.scalar.copy(vrow_t[:, :], row_ps[:, :]).then_inc(s_row_t, 1)

                def key_copy(k, r):
                    act.wait_ge(s_key_ps, k + 1)
                    if not (isinstance(k, int) and k == 0):
                        act.wait_ge(s_prod, k)
                    nc.scalar.copy(key[:, :], key_ps[:, :]).then_inc(s_key, 1)

                def value_copy(k, r):
                    act.wait_ge(s_value_ps, k + 1)
                    nc.scalar.copy(value[:, r % 2, :, 0:HC3], value_ps[:, :].rearrange("p (x c) -> p x c", c=HC3)).then_inc(s_value, 1)

                def rescale(k, r):
                    act.wait_ge(s_drop, k + 1)
                    nc.scalar.activation(scale[:, r % 2, :], drop[:, r % 2, :], ACT.Exp).then_inc(s_scale, 1)

                def group(k, r, first, last):
                    if not last:
                        index(k + U, r)
                    act.wait_ge(s_z, k + 1)
                    nc.scalar.activation(w[:, :], z[:, :, :].rearrange("p j h -> p (j h)"), ACT.Exp).then_inc(s_w, 1)
                    if not (last and r + 2 >= U):
                        for step in (key_rows, turned, value_rows, key_copy, value_copy):
                            step(k + 2, (r + 2) % U)
                    if not (last and r + 1 >= U):
                        rescale(k + 1, (r + 1) % U)
                for r in range(U):
                    index(r, r, False)
                for r in range(2):
                    for step in (key_rows, turned, value_rows, key_copy, value_copy):
                        step(r, r)
                rescale(0, 0)
                groups_loop(act, group)

            @block.tensor
            def _(pe):
                def key_rows(k, r):
                    if not (isinstance(k, int) and k == 0):
                        pe.wait_ge(s_row_t, k * 2)
                    pe.wait_ge(s_krow[r % 2], (k - r) * (16 * G // 2) + (r // 2 + 1) * 16 * G)
                    for j in range(G):
                        mm = pe.transpose(row_ps[:, j * P:(j + 1) * P], krow[:, r % 2, j, :], const["ident"][:, :])
                    mm.then_inc(s_row_ps, 1)

                def turn(k, r):
                    pe.wait_ge(s_hot, k + 1)
                    if not (isinstance(k, int) and k == 0):
                        pe.wait_ge(s_far, k)
                    for j in range(G):
                        mm = pe.transpose(hot_ps[:, j * P:(j + 1) * P], hot[:, r, j, :], const["ident"][:, :])
                    mm.then_inc(s_hot_ps, 1)

                def value_rows(k, r):
                    pe.wait_ge(s_row_t, k * 2 + 1)
                    pe.wait_ge(s_vrow[r % 2], (k - r) * (16 * G // 2) + (r // 2 + 1) * 16 * G)
                    for j in range(G):
                        mm = pe.transpose(row_ps[:, j * P:(j + 1) * P], vrow[:, r % 2, j, :], const["ident"][:, :])
                    mm.then_inc(s_row_ps, 1)

                def project_keys(k, r):
                    if not (isinstance(k, int) and k == 0):
                        pe.wait_ge(s_key, k)
                    for j in range(G):
                        mm = pe.matmul(key_ps[:, j * D:(j + 1) * D], krow_t[:, j * P:(j + 1) * P], wk[:, :], start=True, stop=True)
                    mm.then_inc(s_key_ps, 1)

                def project_values(k, r):
                    pe.wait_ge(s_row_t, k * 2 + 2)
                    if not (isinstance(k, int) and k == 0):
                        pe.wait_ge(s_value, k)
                    for j in range(G):
                        mm = pe.matmul(value_ps[:, j * D:(j + 1) * D], vrow_t[:, j * P:(j + 1) * P], wv[:, :], start=True, stop=True)
                    mm.then_inc(s_value_ps, 1)

                def ask(k, r):
                    pe.wait_ge(s_hot_t, k + 1)
                    pe.wait_ge(s_query, k + 1)
                    if not (isinstance(k, int) and k == 0):
                        pe.wait_ge(s_prod, k)
                    for j in range(G):
                        mm = pe.matmul(query_ps[:, j * D:(j + 1) * D], hot_t[:, r % 2, j * P:(j + 1) * P], query[:, r % 2, :],
                                       start=True, stop=True)
                    mm.then_inc(s_query_ps, 1)

                def spread(k, r, h):
                    if h == 0:
                        pe.wait_ge(s_score, k + 1)
                    if not (isinstance(k, int) and k == 0 and h < 2):
                        pe.wait_ge(s_max, k * H3 + (h - 1))
                    for j in range(G):
                        mm = pe.transpose(spread_ps[:, h % 2, j * P:(j + 1) * P],
                                          score[:, r % 2, j, h:h + 1].to_broadcast([P, P]), const["ident"][:, :])
                    mm.then_inc(s_spread, 1)

                def look_up(k, r):
                    pe.wait_ge(s_new, k + 1)
                    for j in range(G):
                        mm = pe.matmul(new_ps[:, j, :], hot_t[:, r % 2, j * P:(j + 1) * P], new[:, r % 2, :], start=True, stop=True)
                    mm.then_inc(s_new_ps, 1)

                def add_up(k, r):
                    pe.wait_ge(s_msg, k + 1)
                    for j in range(G):
                        mm = pe.matmul(sum_ps, hot[:, r, j, :], msg[:, j * H3:(j + 1) * H3, :].rearrange("p h c -> p (h c)"),
                                       start=(j == 0), stop=(j == G - 1))
                    mm.then_inc(s_sum, 1)

                def group(k, r, first, last):
                    near, r1 = not (last and r + 1 >= U), (r + 1) % U
                    later, r2 = not (last and r + 2 >= U), (r + 2) % U
                    between = {0: key_rows, 1: turn, 2: value_rows, 3: project_keys, 5: ask}
                    for h in range(H3):
                        if near:
                            spread(k + 1, r1, h)
                        if later and h in between:
                            between[h](k + 2, r2)
                        if h == 4:
                            add_up(k, r)
                    if later:
                        project_values(k + 2, r2)
                    if near:
                        look_up(k + 1, r1)
                for r in range(2):
                    for step in (key_rows, turn, value_rows, project_keys, ask, project_values):
                        step(r, r)
                    if r == 0:
                        for h in range(H3):
                            spread(0, 0, h)
                look_up(0, 0)
                groups_loop(pe, group)

            @block.vector
            def _(dve):
                st = Steps(dve, s_step)
                nc.vector.memset(value[:, :, :, HC3], 1.0).then_inc(s_ones, 1)
                dve.wait_ge(s_ones, 1)
                dve.wait_ge(s_slot, 16)

                def one_hot(k, r):
                    nc.vector.tensor_tensor(
                        hot[:, r, :, :], const["lanes"][:, :].unsqueeze(1).to_broadcast([P, G, P]),
                        slot[:, bass.ds(k * G, G), 0].bitcast(F32).unsqueeze(2).to_broadcast([P, G, P]),
                        ALU.is_equal).then_inc(s_hot, 1)

                def block_of(k):
                    return dve.value_load(group_block[0:1, bass.ds(k, 1)], min_val=0, max_val=NB - 1)

                def query_copy(k, r):
                    b = block_of(k)
                    nc.vector.tensor_copy(query[:, r % 2, :], queries[:, bass.ds(b, 1), 0:D].rearrange("p b q -> p (b q)")).then_inc(s_query, 1)

                def products(k, r):
                    dve.wait_ge(s_query_ps, k + 1)
                    dve.wait_ge(s_key, k + 1)
                    nc.vector.tensor_tensor(prod[:, :], query_ps[:, :], key[:, :], ALU.mult).then_inc(s_prod, 1)

                def scores(k, r):
                    dve.wait_ge(s_prod, k + 1)
                    nc.vector.tensor_reduce(score[:, r % 2, :, :].rearrange("p j h -> p (j h)"),
                                            prod[:, :].rearrange("p (x c) -> p x c", c=HC3), AX.X, ALU.add).then_inc(s_score, 1)

                def maximum(k, r, h):
                    if h == 0:
                        dve.wait_ge(s_far, k + 1)
                    dve.wait_ge(s_spread, k * H3 + (h + 1))
                    dve.sem_inc(s_dpast, 1)
                    nc.vector.tensor_tensor_reduce(junk[:, h % 2, :], spread_ps[:, h % 2, :], far[:, r % 2, :], 1.0, -2 * FAR,
                                                   ALU.add, ALU.max, gmax[:, h:h + 1]).then_inc(s_max, 1)

                def new_shift(k, r, b, products_of_next, scores_of_next):
                    at_pass(st, k, 3)
                    shift_b = shift[:, bass.ds(b, 1), :].rearrange("p b h -> p (b h)")
                    bias_b = queries[:, bass.ds(b, 1), D:QW].rearrange("p b h -> p (b h)")
                    products_of_next()
                    dve.wait_ge(s_max, k * H3 + H3)
                    st.did(nc.vector.tensor_tensor(gmax[:, :], gmax[:, :], bias_b, ALU.add))
                    scores_of_next()
                    st.wait()
                    st.did(nc.vector.tensor_tensor(top[:, :], gmax[:, :], shift_b, ALU.max))
                    st.wait()
                    nc.vector.tensor_tensor(new[:, r % 2, :], top[:, :], bias_b, ALU.subtract).then_inc(s_new, 1)
                    nc.vector.tensor_tensor(drop[:, r % 2, :], shift_b, top[:, :], ALU.subtract).then_inc(s_drop, 1)
                    dve.wait_ge(s_drop, k + 1)
                    st.did(nc.vector.tensor_scalar(shift_b, top[:, :], 1.0, None, ALU.mult))
                    st.wait()
                    end_pass(st)

                def logits(k, r):
                    dve.wait_ge(s_new_ps, k + 1)
                    nc.vector.tensor_tensor(z[:, :, :], score[:, r % 2, :, :], new_ps, ALU.subtract).then_inc(s_z, 1)

                def messages(k, r):
                    dve.wait_ge(s_value, k + 1)
                    dve.wait_ge(s_w, k + 1)
                    nc.vector.tensor_tensor(msg[:, :, :], value[:, r % 2, :, :],
                                            w[:, :].unsqueeze(2).to_broadcast([P, G * H3, HC3 + 1]), ALU.mult).then_inc(s_msg, 1)

                def add(k, r, b):
                    dve.wait_ge(s_sum, k + 1)
                    dve.wait_ge(s_scale, k + 1)
                    acc_b = acc[:, bass.ds(b, 1), :].rearrange("p b (h c) -> p (b h) c", h=H3)
                    nc.vector.tensor_tensor(acc_b, acc_b, scale[:, r % 2, :].unsqueeze(2).to_broadcast([P, H3, HC3 + 1]),
                                            ALU.mult).then_inc(s_add, 1)
                    dve.wait_ge(s_add, k * 2 + 1)
                    nc.vector.tensor_tensor(acc_b, acc_b, sum_ps.rearrange("p (h c) -> p h c", h=H3),
                                            ALU.add).then_inc(s_add, 1)
                    dve.wait_ge(s_add, k * 2 + 2)

                blocks = {}

                def group(k, r, first, last):
                    if r == 0:
                        blocks.clear()
                    near, r1 = not (last and r + 1 >= U), (r + 1) % U
                    later, r2 = not (last and r + 2 >= U), (r + 2) % U
                    logits(k, r)
                    for h in range(H3):
                        if near:
                            maximum(k + 1, r1, h)
                        if h == 0 and not (first and r == 0):
                            add(k - 1, (r - 1) % U, blocks[r - 1] if r else block_of(k - 1))
                        if h == 1:
                            messages(k, r)
                        if h == 3 and not (last and r + 3 >= U):
                            one_hot(k + 3, (r + 3) % U)
                            query_copy(k + 3, (r + 3) % U)
                        if h == 5 and near:
                            blocks[r + 1] = block_of(k + 1)
                        if h == 6 and r not in blocks:
                            blocks[r] = block_of(k)
                    if near:
                        new_shift(k + 1, r1, blocks[r + 1], lambda: later and products(k + 2, r2),
                                  lambda: later and scores(k + 2, r2))
                for r in range(3):
                    one_hot(r, r)
                query_copy(0, 0)
                query_copy(1, 1)
                products(0, 0)
                scores(0, 0)
                for h in range(H3):
                    maximum(0, 0, h)
                new_shift(0, 0, block_of(0), lambda: products(1, 1), lambda: scores(1, 1))
                query_copy(2, 2)
                groups_loop(dve, group)
                add(NG - 1, U - 1, block_of(NG - 1))


def attention_finish(nc, const, tag, x, h, acc, bv, wo, bo):
    with Phase(nc) as ctx:
        sb, pb, sem = memory(nc, ctx, tag)
        rec = sb("rec", [P, NB, H3])
        bvr = sb("bvr", [P, D])
        row = sb("row", [1, D])
        proj = Project(nc, ctx, const, tag + "proj", h, wo[:, :], row[:, :], D, 3)
        s_v, s_in, s_bv = sem("vector_step"), sem("loaded"), sem("bias_loaded")
        with nc.Block() as block:
            @block.sync
            def _(sp):
                sp.dma_start(row[:, :], bo.rearrange("(o d) -> o d", o=1)).then_inc(s_in, 16)
                sp.dma_start(bvr[:, :], bv.rearrange("(o d) -> o d", o=1).to_broadcast([P, D])).then_inc(s_bv, 16)

            @block.tensor
            def _(pe):
                pe.wait_ge(s_in, 16)
                proj.tensor(pe)

            @block.scalar
            def _(act):
                proj.scalar(act)

            @block.vector
            def _(dve):
                st = Steps(dve, s_v)
                dve.wait_ge(s_bv, 16)
                a = acc[:, :, :].rearrange("p b (h c) -> p b h c", h=H3)
                hv = h[:, :, :].rearrange("p b (h c) -> p b h c", h=H3)
                bvh = bvr[:, :].rearrange("p (h c) -> p h c", h=H3)
                for t in range(H3):
                    st.did(nc.vector.tensor_tensor(hv[:, :, t, :], a[:, :, t, HC3:HC3 + 1].to_broadcast([P, NB, HC3]),
                                                   bvh[:, t, :].unsqueeze(1).to_broadcast([P, NB, HC3]), ALU.mult))
                st.wait()
                for t in range(H3):
                    st.did(nc.vector.tensor_tensor(hv[:, :, t, :], hv[:, :, t, :], a[:, :, t, 0:HC3], ALU.add))
                st.did(nc.vector.tensor_scalar(rec[:, :, :], a[:, :, :, HC3], 1e-16, None, ALU.add))
                st.wait()
                st.did(nc.vector.reciprocal(rec[:, :, :], rec[:, :, :]))
                st.wait()
                hf = h[:, :, :].rearrange("p b (h c) -> p (b h) c", h=H3)
                st.did(nc.vector.tensor_tensor(hf, hf, rec[:, :, :].rearrange("p b h -> p (b h)").unsqueeze(2).to_broadcast([P, NB * H3, HC3]), ALU.mult))
                st.wait()
                dve.sem_inc(proj.s_h, 1)
                into_x(nc, proj, dve, x)


def program(nc, a, out):
    with Phase(nc) as ctx:
        const = constants(nc, ctx)
        sb, pb, sem = memory(nc, ctx)
        by_target = nc.dram_tensor("by_target", (SLOTS + PADS, 4), I32).ap()
        target_groups = sb("target_groups", [P, NG], I32)
        source_groups = sb("source_groups", [P, NG], I32)
        bucket_edges(nc, const, "t_", a["dst"], a["src"], by_target, target_groups)
        by_source = nc.dram_tensor("by_source", (SLOTS + PADS, 4), I32).ap()
        bucket_edges(nc, const, "s_", a["src"], a["dst"], by_source, source_groups)

        x = sb("x", [P, NB, D])
        h = sb("h", [P, NB, D])
        wx, bx = sb("wx", [P, WX]), sb("bx", [1, WX])
        tables = [nc.dram_tensor(f"table{n}", (NODES, TABW), F32).ap() for n in range(3)]
        h_rows = nc.dram_tensor("h_rows", (NODES, D), F32).ap()
        load_x(nc, a["x"], x)
        with Phase(nc) as gat:
            sb, pb, sem = memory(nc, gat, "gat_")
            ed, shift = sb("ed", [P, NB, H]), sb("shift", [P, NB, H])
            acc = sb("acc", [P, NB, ROW])
            gat_weights(nc, const, "w0f_", a["L0_gnn_W1"], a["L0_gnn_a_src1"], a["L0_gnn_a_dst1"], wx, bx)
            gat_nodes(nc, const, "n0f_", x, h, wx, bx, tables[0], ed, shift, acc, True)
            gat_edges(nc, const, "e0f_", by_target, target_groups, tables[0], ed, shift, acc)
            gat_finish(nc, "f0f_", x, acc, True, (a["L0_gnn_b1"],))
            gat_weights(nc, const, "w0b_", a["L0_gnn_W2"], a["L0_gnn_a_src2"], a["L0_gnn_a_dst2"], wx, bx)
            gat_nodes(nc, const, "n0b_", None, h, wx, bx, tables[1], ed, shift, acc, True)
            gat_edges(nc, const, "e0b_", by_source, source_groups, tables[1], ed, shift, acc)
            gat_finish(nc, "f0b_", x, acc, True, (a["L0_gnn_b2"],))
            w1, total = sb("w1", [P, D]), sb("total", [P, D])
            turned_weights(nc, const, "w1_", [(a["L1_gnn_W"], w1[:, :])])
            complement_nodes(nc, "n1_", x, h, h_rows, acc, const, total)
            sum_edges(nc, const, "e1_", by_target, target_groups, h_rows, acc)
            complement_finish(nc, const, "f1_", x, h, acc, total, w1, a["L1_gnn_b"])
            gat_weights(nc, const, "w2_", a["L2_gnn_lin_weight"], a["L2_gnn_att_src"], a["L2_gnn_att_dst"], wx, bx,
                        a["L2_gnn_coeffs_t"], a["L2_gnn_lin_bias"])
            gat_nodes(nc, const, "n2_", x, h, wx, bx, tables[2], ed, shift, acc, False)
            gat_edges(nc, const, "e2_", by_target, target_groups, tables[2], ed, shift, acc)
            gat_finish(nc, "f2_", x, acc, False)
        with Phase(nc) as att:
            sb, pb, sem = memory(nc, att, "att_")
            wk, wv, wo, qx, qb = sb("wk", [P, D]), sb("wv", [P, D]), sb("wo", [P, D]), sb("qx", [P, QW]), sb("qb", [1, QW])
            queries, shift, acc = sb("queries", [P, NB, QW]), sb("shift", [P, NB, H3]), sb("acc", [P, NB, ROW3])
            turned_weights(nc, const, "w3_", [(a["L3_gnn_Wk"], wk[:, :]), (a["L3_gnn_Wv"], wv[:, :]), (a["L3_gnn_Wo"], wo[:, :])])
            query_weights(nc, const, "wq_", a["L3_gnn_Wq"], a["L3_gnn_bq"], a["L3_gnn_bk"], qx, qb)
            attention_nodes(nc, const, "n3_", x, h, qx, qb, queries, shift, acc)
            attention_edges(nc, const, "e3_", by_source, source_groups, a["edge_attr_128"], a["edge_attr_128_n2"],
                            wk, wv, queries, shift, acc)
            attention_finish(nc, const, "f3_", x, h, acc, a["L3_gnn_bv"], wo, a["L3_gnn_bo"])
        store_x(nc, out, x)


_INS = ['x', 'src', 'dst', 'edge_attr_128', 'edge_attr_128_n2',
        'L0_gnn_W1', 'L0_gnn_a_src1', 'L0_gnn_a_dst1', 'L0_gnn_b1', 'L0_gnn_W2', 'L0_gnn_a_src2', 'L0_gnn_a_dst2',
        'L0_gnn_b2', 'L1_gnn_W', 'L1_gnn_b', 'L2_gnn_coeffs_t', 'L2_gnn_lin_weight', 'L2_gnn_lin_bias',
        'L2_gnn_att_src', 'L2_gnn_att_dst', 'L3_gnn_Wq', 'L3_gnn_bq', 'L3_gnn_Wk', 'L3_gnn_bk', 'L3_gnn_Wv',
        'L3_gnn_bv', 'L3_gnn_Wo', 'L3_gnn_bo']


def kernel(**inputs):
    import numpy as _np
    import concourse.bacc as _bacc
    from concourse import mybir as _mybir
    from concourse.bass_utils import run_bass_kernel_spmd as _run

    nc = _bacc.Bacc("TRN2", target_bir_lowering=False, num_devices=1)
    arrays, args = {}, {}
    for name in _INS:
        a = _np.ascontiguousarray(inputs[name])
        arrays[f"in_{name}"] = a
        args[name] = nc.dram_tensor(f"in_{name}", a.shape, _mybir.dt.from_np(a.dtype), kind="ExternalInput").ap()
    out = nc.dram_tensor("out", (N, D), _mybir.dt.float32, kind="ExternalOutput").ap()
    program(nc, args, out)
    return _run(nc, [arrays], core_ids=[0]).results[0]["out"]
```
